# Optimizing a Trainium2 kernel written in Bass

```python
import numpy as np
import jax
import jax.numpy as jnp

def _softmax(x, axis=-1):
    return jax.nn.softmax(x, axis=axis)

def _gelu(x):
    return jax.nn.gelu(x, approximate=True)

def _silu(x):
    return jax.nn.silu(x)

def _sigmoid(x):
    return jax.nn.sigmoid(x)

def _layernorm(x, axis=-1, eps=1e-05):
    m = jnp.mean(x, axis=axis, keepdims=True)
    v = jnp.var(x, axis=axis, keepdims=True)
    return (x - m) / jnp.sqrt(v + eps)

def _scatter_add(tgt, idx, src, axis=0):
    return tgt.at[idx].add(src)

def _segment_sum(src, seg, n):
    return jax.ops.segment_sum(src, seg, n)
kernel_name = 'mk_prb_d1_jaxref_r4_8826d1'

def setup_inputs(seed: int=0):
    np.random.seed(seed)
    _w = jnp.asarray

    def _L0_attn_setup():
        import jax, jax.numpy as jnp
        import numpy as np
        DT_RANK = 64
        D_STATE = 16
        DIM_INNER = 256
        IN_FEATURES = 256

        def _combine(c1, c2):
            a1, b1 = c1
            a2, b2 = c2
            return (a1 * a2, a2 * b1 + b2)
        key = jax.random.key(seed)
        ks = jax.random.split(key, 4)
        B, L = (4, 512)
        x = jax.random.normal(ks[0], (B, L, IN_FEATURES), dtype=jnp.float32)
        W_deltaBC = jax.random.normal(ks[1], (DT_RANK + 2 * D_STATE, IN_FEATURES), dtype=jnp.float32) / np.sqrt(IN_FEATURES)
        W_dt = jax.random.normal(ks[2], (DIM_INNER, DT_RANK), dtype=jnp.float32) / np.sqrt(DT_RANK)
        b_dt = jax.random.normal(ks[3], (DIM_INNER,), dtype=jnp.float32) * 0.01
        A_log = jnp.log(jnp.tile(jnp.arange(1, D_STATE + 1, dtype=jnp.float32), (DIM_INNER, 1)))
        D_param = jnp.ones((DIM_INNER,), dtype=jnp.float32)
        return {'x': x, 'W_deltaBC': W_deltaBC, 'W_dt': W_dt, 'b_dt': b_dt, 'A_log': A_log, 'D_param': D_param}
    _L0_attn_in = _L0_attn_setup()

    def _L0_ffn_setup():
        import jax, jax.numpy as jnp
        import numpy as np
        B, S, H, E, K, F = (4, 512, 256, 8, 128, 1024)
        key = jax.random.key(seed)
        k0, k1, k2, k3 = jax.random.split(key, 4)
        sc = lambda d: 1.0 / np.sqrt(d).astype(np.float32)
        return {'x': jax.random.normal(k0, (B, S, H), jnp.float32), 'Wg': jax.random.normal(k1, (E, H), jnp.float32) * sc(H), 'W1': jax.random.normal(k2, (E, H, F), jnp.float32) * sc(H), 'b1': jnp.zeros((E, F), jnp.float32), 'W2': jax.random.normal(k3, (E, F, H), jnp.float32) * sc(F), 'b2': jnp.zeros((E, H), jnp.float32)}
    _L0_ffn_in = _L0_ffn_setup()
    _d = {'L0_attn_x': _L0_attn_in['x'], 'L0_attn_W_deltaBC': _L0_attn_in['W_deltaBC'], 'L0_attn_W_dt': _L0_attn_in['W_dt'], 'L0_attn_b_dt': _L0_attn_in['b_dt'], 'L0_attn_A_log': _L0_attn_in['A_log'], 'L0_attn_D_param': _L0_attn_in['D_param'], 'L0_ffn_Wg': _L0_ffn_in['Wg'], 'L0_ffn_W1': _L0_ffn_in['W1'], 'L0_ffn_b1': _L0_ffn_in['b1'], 'L0_ffn_W2': _L0_ffn_in['W2'], 'L0_ffn_b2': _L0_ffn_in['b2']}
    _x0 = _d['L0_attn_x']
    _d['L0_attn_x'] = jax.random.normal(jax.random.fold_in(jax.random.key(seed), 1), (32, 512, 256), dtype=_x0.dtype)
    del _x0
    return _d

def reference(L0_attn_x, L0_attn_W_deltaBC, L0_attn_W_dt, L0_attn_b_dt, L0_attn_A_log, L0_attn_D_param, L0_ffn_Wg, L0_ffn_W1, L0_ffn_b1, L0_ffn_W2, L0_ffn_b2):

    def _L0_attn_ref(x, W_deltaBC, W_dt, b_dt, A_log, D_param):
        import jax, jax.numpy as jnp
        import numpy as np
        DT_RANK = 64
        D_STATE = 16
        DIM_INNER = 256
        IN_FEATURES = 256

        def _combine(c1, c2):
            a1, b1 = c1
            a2, b2 = c2
            return (a1 * a2, a2 * b1 + b2)
        deltaBC = x @ W_deltaBC.T
        delta, Bmat, Cmat = jnp.split(deltaBC, [DT_RANK, DT_RANK + D_STATE], axis=-1)
        delta = jax.nn.softplus(delta @ W_dt.T + b_dt)
        A = -jnp.exp(A_log)
        D = D_param
        deltaA = jnp.exp(delta[..., None] * A)
        BX = delta[..., None] * Bmat[:, :, None, :] * x[..., None]
        _, hs = jax.lax.associative_scan(_combine, (deltaA, BX), axis=1)
        y = jnp.einsum('blds,bls->bld', hs, Cmat) + D * x
        return y

    def _L0_ffn_ref(x, Wg, W1, b1, W2, b2):
        import jax, jax.numpy as jnp
        import numpy as np
        B, S, H, E, K, F = (4, 512, 256, 8, 128, 1024)
        b, s, h = x.shape
        logits = jnp.einsum('bsh,eh->bse', x, Wg)
        Sm = jnp.swapaxes(jax.nn.softmax(logits, axis=-1), 1, 2)
        G, I = jax.lax.top_k(Sm, K)
        ex = jnp.take_along_axis(x[:, None, :, :], I[..., None], axis=2)
        h1 = jax.nn.gelu(jnp.einsum('bekh,ehf->bekf', ex, W1) + b1[None, :, None, :])
        out = jnp.einsum('bekf,efh->bekh', h1, W2) + b2[None, :, None, :]
        out = G[..., None] * out
        new_x = jnp.zeros_like(x).at[jnp.arange(b)[:, None, None], I].add(out)
        return new_x
    x = L0_attn_x
    xn = _layernorm(x, axis=-1)
    x = x + _L0_attn_ref(xn, L0_attn_W_deltaBC, L0_attn_W_dt, L0_attn_b_dt, L0_attn_A_log, L0_attn_D_param) + _L0_ffn_ref(xn, L0_ffn_Wg, L0_ffn_W1, L0_ffn_b1, L0_ffn_W2, L0_ffn_b2)
    return x

_drawn_inputs = setup_inputs


def setup_inputs(seed=0):
    import zlib

    import numpy as np

    out = dict(_drawn_inputs(seed))
    spreads = {'L0_attn_D_param': (1.0, 0.2), 'L0_ffn_b1': (0.0, 0.8), 'L0_ffn_b2': (0.0, 0.764)}
    factors = {'L0_attn_b_dt': 8.0}
    for name, (base, spread) in spreads.items():
        noise = np.random.default_rng([zlib.crc32(name.encode()), seed]).standard_normal(out[name].shape)
        drawn = base * np.exp(spread * noise) if base else spread * noise
        out[name] = jnp.asarray(drawn.astype(out[name].dtype))
    for name, factor in factors.items():
        out[name] = (out[name] * factor).astype(out[name].dtype)
    return out
```

```python
import numpy as np
import concourse.bass as bass
from concourse import mybir
from contextlib import ExitStack

F32 = mybir.dt.float32
BF16 = mybir.dt.bfloat16
U32 = mybir.dt.uint32
I32 = mybir.dt.int32
ALU = mybir.AluOpType
ACT = mybir.ActivationFunctionType
AX = mybir.AxisListType

P = 128
NB, T, D = 32, 512, 256
R, N = 64, 16
E, K, F = 8, 128, 1024
TC, HC, FC = T // P, D // P, F // P
BC = R + 2 * N
HALF = NB // 2
UB = 2
UT = UB * K
SLOTS = 4
STEPS = N // SLOTS
BODY = 4
BU = BODY * SLOTS
NJ = NB // BODY
NU = NB * SLOTS
EPS = 1e-5


def wait(eng, sem, value):
    if not (isinstance(value, int) and value <= 0):
        eng.wait_ge(sem, value)


def there(index, count):
    return not isinstance(index, int) or 0 <= index < count


def build(nc, x, wdbc, wdt, bdt, alog, dpar, wg, w1, b1, w2, b2, out):
    ctx = ExitStack()
    with ctx:
        def sb(name, shape, dt=F32):
            return ctx.enter_context(nc.sbuf_tensor(name, shape, dt))

        def bank(name):
            return ctx.enter_context(nc.psum_tensor(name, [P, 512], F32))

        def sem(name):
            return ctx.enter_context(nc.semaphore(name))

        xn_rows = nc.dram_tensor("xn_rows", [NB * T, D], F32, kind="Internal").ap()
        xn_cols = nc.dram_tensor("xn_cols", [NB, P, HC, T], F32, kind="Internal").ap()
        x_tiles = x.rearrange("b (c p) d -> b p c d", p=P)
        out_rows = out.rearrange("b t d -> (b t) d")
        out_tiles = out.rearrange("b (c p) d -> b p c d", p=P)
        xn_tiles = xn_rows.rearrange("(b c p) d -> b p c d", p=P, c=TC)
        w1_tiles = w1.rearrange("e (c p) f -> e p c f", p=P)
        w2_tiles = w2.rearrange("e (c p) d -> e p c d", p=P)

        ident = sb("ident", [P, P])
        sel = sb("sel", [3 * 2 * N, 2 * N, P], BF16)
        ones3 = sb("ones3", [3, P], BF16)
        neg_half = sb("neg_half", [P, TC])
        wdbc_sb = sb("wdbc_sb", [P, HC, BC])
        wdt_sb = sb("wdt_sb", [R, D])
        bdt_sb = sb("bdt_sb", [P, HC])
        a_sb = sb("a_sb", [P, HC, N])
        dpar_sb = sb("dpar_sb", [P, HC])
        wg_sb = sb("wg_sb", [P, HC, E])
        b1_all = sb("b1_all", [P, 2, E * FC])
        b1_st = sb("b1_st", [P, 2, FC])
        b2_all = sb("b2_all", [3, 2 * E * D], BF16)
        b2_st = sb("b2_st", [3, 2, D], BF16)
        w1_sb = sb("w1_sb", [P, 2, HC, F])
        w2_sb = sb("w2_sb", [P, 2, FC, D])
        decay = sb("decay", [P, 2, STEPS, HC, T])
        xnt = sb("xnt", [P, 2, HC, T])
        delta = sb("delta", [P, 2, HC, T])
        du = sb("du", [P, 2, HC, T])
        skip = sb("skip", [P, 2, HC, T])
        state = sb("state", [P, 2, HC, T])
        prod = sb("prod", [P, 4, HC, T])
        ysum = sb("ysum", [P, 2, HC, T])
        zabs = sb("zabs", [P, HC, T])
        zpos = sb("zpos", [P, HC, T])
        yrow = sb("yrow", [P, TC, D])
        low = sb("low", [R, T])
        bc_hi = sb("bc_hi", [P, T], BF16)
        bc_mid = sb("bc_mid", [P, T], BF16)
        bc_rest = sb("bc_rest", [P, T])
        bcs = sb("bcs", [3 * 2 * N, 2, T], BF16)
        ex = sb("ex", [P, 2, UB, D])
        ext = sb("ext", [P, 2, HC, UT])
        hid = sb("hid", [P, 2, FC, UT])
        og = sb("og", [P, 2, UB, D])
        idx_all = sb("idx_all", [P, 2 * P], U32)
        gate_all = sb("gate_all", [P, 2 * P])
        idx_st = sb("idx_st", [P, BODY, 8], U32)
        gate_st = sb("gate_st", [P, BODY, 8])
        dflat = decay[:, :, :, :, :].rearrange("p a b c t -> p (a b c t)")
        xin = dflat[:, 0:4 * 1024].rearrange("p (r c d) -> p r c d", r=4, c=TC)
        xno = dflat[:, 4 * 1024:8 * 1024].rearrange("p (r c d) -> p r c d", r=4, c=TC)
        xtr = delta[:, :, :, :]
        stats = sb("stats", [P, 4, TC, 6])
        mv = sb("mv", [P, 4, TC, 2])
        vare = sb("vare", [P, 4, TC])
        rstd = sb("rstd", [P, 4, TC])
        lmax = sb("lmax", [P, 4, TC])
        lsh = sb("lsh", [P, 4, TC, E])
        lexp = sb("lexp", [P, 4, TC, E])
        lsum = sb("lsum", [P, 4, TC])
        lrec = sb("lrec", [P, 4, TC])
        probs = sb("probs", [P, TC, NB, E])
        work = prod[:, 0, :, :]
        vals = sb("vals", [P, 2, K])
        idx_u = sb("idx_u", [P, 2, K], U32)
        idx_f = sb("idx_f", [P, 2, K])
        row_i = sb("row_i", [P, 2], I32)
        row_f = sb("row_f", [P, 2])
        b2_f = prod[0:1, 1:3, :, :].rearrange("p a b t -> p (a b t)")
        b2_r = prod[0:1, 3:4, :, :]
        b2_hi = ysum[0:1, 0, :, :].rearrange("p c t -> p (c t)").bitcast(BF16)
        b2_mid = ysum[0:1, 1, :, :].rearrange("p c t -> p (c t)").bitcast(BF16)
        b2_lo = yrow[0:1, :, :].rearrange("p c t -> p (c t)").bitcast(BF16)

        bank_b, bank_x, bank_c, bank_o = bank("bank_b"), bank("bank_x"), bank("bank_c"), bank("bank_o")
        bank_l = [bank(f"bank_l{i}") for i in range(4)]

        params_in = sem("params_in")
        b1_in = sem("b1_in")
        ident_made = sem("ident_made")
        sel_made = sem("sel_made")
        row_made = sem("row_made")
        consts_set = sem("consts_set")
        a_exp = sem("a_exp")
        a_made = sem("a_made")
        b2_step = sem("b2_step")
        b2_moved = sem("b2_moved")
        x_in = [sem(f"x_in{i}") for i in range(4)]
        resid_out = [sem(f"resid_out{i}") for i in range(4)]
        rows_out = [sem(f"rows_out{i}") for i in range(4)]
        cols_out = [sem(f"cols_out{i}") for i in range(2)]
        stats_done = sem("stats_done")
        mv_done = sem("mv_done")
        vare_done = sem("vare_done")
        rstd_done = sem("rstd_done")
        xn_done = sem("xn_done")
        xn_tr = sem("xn_tr")
        xnt_done = sem("xnt_done")
        logits_done = sem("logits_done")
        lmax_done = sem("lmax_done")
        lsh_done = sem("lsh_done")
        lexp_done = sem("lexp_done")
        lnorm = sem("lnorm")
        probs_done = sem("probs_done")
        probs_tr = sem("probs_tr")
        work_in = sem("work_in")
        round_op = sem("round_op")
        picks = sem("picks")
        picks_tr = sem("picks_tr")
        picks_done = sem("picks_done")
        xnt_in = [sem(f"xnt_in{i}") for i in range(2)]
        bc_proj = sem("bc_proj")
        hi_done = sem("hi_done")
        low_done = sem("low_done")
        rest_done = sem("rest_done")
        mid_done = sem("mid_done")
        lo_done = sem("lo_done")
        hi_moved = sem("hi_moved")
        mid_moved = sem("mid_moved")
        z_done = sem("z_done")
        z_taken = sem("z_taken")
        sp_step = sem("sp_step")
        delta_done = sem("delta_done")
        du_done = sem("du_done")
        skip_done = sem("skip_done")
        decay_done = sem("decay_done")
        b_ready = sem("b_ready")
        c_ready = sem("c_ready")
        bx_done = sem("bx_done")
        scan_done = sem("scan_done")
        prod_done = sem("prod_done")
        sum_done = sem("sum_done")
        y_tr = sem("y_tr")
        yrow_done = sem("yrow_done")
        y_added = sem("y_added")
        w1_in = [sem(f"w1_in{i}") for i in range(2)]
        w2_in = [sem(f"w2_in{i}") for i in range(2)]
        staged = sem("staged")
        gates_staged = sem("gates_staged")
        idx_staged = sem("idx_staged")
        gathered = [sem(f"gathered{i}") for i in range(2)]
        ex_tr = sem("ex_tr")
        ext_done = sem("ext_done")
        up_done = sem("up_done")
        gelu_done = sem("gelu_done")
        down_done = sem("down_done")
        og_done = sem("og_done")
        scattered = sem("scattered")
        turn = {name: sem(f"turn_{name}") for name in ("sp", "pool", "dve")}

        def both(emit, count):
            def run(eng):
                emit(0)
                with eng.Fori(1, count - 1) as i:
                    emit(i)
                emit(count - 1)
                emit(count)
            return run

        block = ctx.enter_context(nc.Block())

        @block.sync
        def _(sp):
            def held(sem, value):
                wait(sp, sem, value)
                if not isinstance(value, int):
                    sp.sem_inc(turn["sp"], 1)

            for dst, src in ((wdbc_sb[:], wdbc.rearrange("(c p) m -> p c m", p=P)), (wdt_sb[:], wdt),
                             (bdt_sb[:], bdt), (a_sb[:], alog), (dpar_sb[:], dpar),
                             (wg_sb[:], wg.rearrange("(c p) e -> p c e", p=P)), (b2_f, b2)):
                sp.dma_start(dst, src).then_inc(params_in, 16)
            for half in range(2):
                sp.dma_start(b1_all[:, half], b1).then_inc(b1_in, 16)

            def rows(q):
                for r in range(4):
                    b = q * 4 + r
                    if there(b, NB):
                        held(xn_done, q * 4 + r - 3)
                        held(resid_out[r], q * 16)
                        sp.dma_start(xin[:, r], x_tiles[b]).then_inc(x_in[r], 16)
                    r2 = (r - 2) % 4
                    if there(b - 2, NB):
                        held(x_in[r2], (q + (0 if r >= 2 else -1)) * 16 + 16)
                        sp.dma_start(out_tiles[b - 2], xin[:, r2]).then_inc(resid_out[r2], 16)

            both(rows, NB // 4)(sp)

            held(b2_step, 5)
            for half in range(2):
                for row, part in enumerate((b2_hi, b2_mid, b2_lo)):
                    sp.dma_start(b2_all[row:row + 1, half * E * D:(half + 1) * E * D], part[:]).then_inc(b2_moved, 16)

            def load_weights(e, par, w1_free, w2_free):
                held(up_done, w1_free)
                sp.dma_start(w1_sb[:, par], w1_tiles[e]).then_inc(w1_in[par], 16)
                held(down_done, w2_free)
                sp.dma_start(w2_sb[:, par], w2_tiles[e]).then_inc(w2_in[par], 16)

            load_weights(0, 0, 0, 0)
            for r in range(4):
                held(resid_out[r], 16 * NB // 4)
                held(rows_out[r], 16 * NB // 4)
            for r in range(2):
                held(cols_out[r], 16 * NB // 2)
            for b in range(2):
                sp.dma_start(xnt[:, b], xn_cols[b]).then_inc(xnt_in[b], 16)

            def move_parts(nb, par, used):
                held(hi_done, nb)
                held(c_ready, used)
                sp.dma_start(bcs[0:32, par], bc_hi[64:96, :]).then_inc(hi_moved, 16)
                held(mid_done, nb)
                sp.dma_start(bcs[32:64, par], bc_mid[64:96, :]).then_inc(mid_moved, 16)

            move_parts(1, 0, 0)

            def main(j):
                for m in range(BODY):
                    b = j * BODY + m
                    if not there(b, NB):
                        continue
                    if there(b + 2, NB):
                        held(du_done, b + 1)
                        held(skip_done, b + 1)
                        held(bc_proj, b + 1)
                        sp.dma_start(xnt[:, m % 2], xn_cols[b + 2]).then_inc(xnt_in[m % 2], 16)
                    if m == 0:
                        load_weights((j * 2 + 1) % E, 1, j * BU * 4, j * BU)
                    if m == 2 and there(j + 1, NJ):
                        load_weights((j * 2 + 2) % E, 0, j * BU * 4 + BU * 2, j * BU + BU // 2)
                    if there(b + 1, NB):
                        move_parts(b + 2, (m + 1) % 2, b * N)

            both(main, NJ)(sp)
            held(y_added, 16 * NB)
            held(scattered, 32 * NU)

        @block.gpsimd
        def _(pool):
            nc.gpsimd.memset(ident[:], 0.0).then_inc(ident_made, 1)
            nc.gpsimd.memset(neg_half[:], -0.5).then_inc(consts_set, 1)
            pool.wait_ge(ident_made, 1)
            nc.gpsimd.affine_select(out=ident[:], in_=ident[:], compare_op=ALU.not_equal, fill=1.0, base=0,
                                    pattern=[[-1, P]], channel_multiplier=1).then_inc(ident_made, 1)
            nc.gpsimd.iota(row_i[:, 0:1], pattern=[[0, 1]], base=0, channel_multiplier=1).then_inc(row_made, 1)
            nc.gpsimd.memset(sel[:], 0.0).then_inc(sel_made, 1)
            for part in range(3):
                pool.wait_ge(sel_made, part + 1)
                nc.gpsimd.affine_select(out=sel[:], in_=sel[:], compare_op=ALU.not_equal, fill=1.0,
                                        base=-32 * part, pattern=[[-1, 2 * N], [0, P]],
                                        channel_multiplier=1).then_inc(sel_made, 1)

            def rows(q):
                for r in range(4):
                    b = q * 4 + r
                    if there(b, NB):
                        pool.wait_ge(vare_done, b + 1)
                        nc.gpsimd.tensor_tensor(rstd[:, r], vare[:, r], neg_half[:], ALU.pow).then_inc(rstd_done, 1)
                    if there(b - 1, NB):
                        r1 = (r - 1) % 4
                        pool.wait_ge(xn_done, b)
                        pool.dma_start(xn_tiles[b - 1], xno[:, r1]).then_inc(rows_out[r1], 16)

            both(rows, NB // 4)(pool)
            for r in range(4):
                pool.wait_ge(resid_out[r], 16 * NB // 4)
                pool.wait_ge(rows_out[r], 16 * NB // 4)

            def stage_idx(m, col):
                nc.gpsimd.tensor_copy(idx_st[:, m], idx_all[:, bass.ds(col, 8)]).then_inc(idx_staged, 1)

            def gather(k, sl, m, passes, ga_free):
                wait(pool, ex_tr, ga_free)
                pool.wait_ge(idx_staged, passes)
                pool.sem_inc(turn["pool"], 1)
                for i in range(UB):
                    pool.indirect_dma_start(
                        out=ex[:, k % 2, i], out_offset=None, in_=xn_rows,
                        in_offset=bass.IndirectOffsetOnAxis(ap=idx_st[:, m, 2 * sl + i:2 * sl + i + 1], axis=0),
                    ).then_inc(gathered[k % 2], 16)

            pool.wait_ge(b2_moved, 16 * 6)
            pool.wait_ge(picks_done, 4)
            stage_idx(0, 0)
            gather(0, 0, 0, 1, 0)
            gather(1, 1, 0, 1, 0)

            def main(j):
                for k in range(BU):
                    m, sl = k // SLOTS, k % SLOTS
                    u, b = j * BU + k, j * BODY + m
                    for i in range(STEPS):
                        n = sl * STEPS + i
                        s = b * N + n
                        if there(b, NB):
                            pool.wait_ge(prod_done, s * 2 + 2)
                            if n == 0:
                                pool.wait_ge(skip_done, b + 1)
                                wait(pool, y_tr, b - 1)
                                first = skip[:, m % 2]
                            else:
                                pool.wait_ge(sum_done, s)
                                first = ysum[:, m % 2]
                            nc.gpsimd.tensor_tensor(ysum[:, m % 2], first, prod[:, i], ALU.add).then_inc(sum_done, 1)
                        if i == 0:
                            if sl == 2 and there(b + 1, NB):
                                wait(pool, scattered, u * 32 - 64 * 2)
                                stage_idx((m + 1) % BODY, b * 8 + 8)
                            if there(u + 2, NU):
                                nm = ((k + 2) // SLOTS) % BODY
                                gather(k, (sl + 2) % SLOTS, nm, b + (2 if sl >= 2 else 1), u + 1)
                        if i in (1, 2) and there(u - 2, NU):
                            c = i - 1
                            sm = ((k - 2) // SLOTS) % BODY
                            pool.wait_ge(og_done, u * 2 - 2)
                            wait(pool, scattered, u * 32 - 64 + 16 * c)
                            wait(pool, y_added, b * 16 - 16)
                            so = 2 * ((sl + 2) % SLOTS) + c
                            pool.sem_inc(turn["pool"], 1)
                            pool.indirect_dma_start(
                                out=out_rows,
                                out_offset=bass.IndirectOffsetOnAxis(ap=idx_st[:, sm, so:so + 1], axis=0),
                                in_=og[:, k % 2, c], in_offset=None, compute_op=ALU.add,
                            ).then_inc(scattered, 16)
                        if i == 3 and sl == 3 and there(b - 1, NB):
                            pool.wait_ge(yrow_done, b * 2)
                            if isinstance(u, int):
                                pool.wait_ge(scattered, 32 * min(u - 1, NU))
                            else:
                                pool.wait_ge(scattered, u * 32 - 32)
                            pool.dma_start(out_tiles[b - 1], yrow[:], accum_op=ALU.add).then_inc(y_added, 16)

            both(main, NJ)(pool)

        @block.scalar
        def _(act):
            act.wait_ge(params_in, 16 * 7)
            nc.scalar.activation(a_sb[:], a_sb[:], ACT.Exp).then_inc(a_exp, 1)

            def rows(q):
                for r in range(4):
                    b = q * 4 + r
                    par = r % 2
                    if there(b - 3, NB):
                        act.wait_ge(lsh_done, b - 2)
                        nc.scalar.activation(lexp[:, (r - 3) % 4], lsh[:, (r - 3) % 4], ACT.Exp).then_inc(lexp_done, 1)
                    if there(b, NB):
                        act.wait_ge(xn_tr, b + 1)
                        wait(act, cols_out[par], (q * 2 + r // 2) * 16)
                        wait(act, logits_done, b - 1)
                        for hc in range(HC):
                            nc.scalar.copy(xtr[:, par, hc], bank_l[2 * par + hc][:]).then_inc(xnt_done, 1)
                        act.wait_ge(xnt_done, b * 2 + 2)
                        act.dma_start(xn_cols[b], xtr[:, par]).then_inc(cols_out[par], 16)

            both(rows, NB // 4)(act)

            def take_bc(nb):
                act.wait_ge(bc_proj, nb)
                wait(act, hi_moved, nb * 16 - 16)
                nc.scalar.copy(bc_hi[64:96, :], bank_l[3][64:96, :]).then_inc(hi_done, 1)
                wait(act, z_done, nb - 1)
                nc.scalar.copy(low[:], bank_l[3][0:R, :]).then_inc(low_done, 1)

            def take_mid(nb):
                act.wait_ge(rest_done, nb)
                wait(act, mid_moved, nb * 16 - 16)
                wait(act, lo_done, nb - 1)
                nc.scalar.copy(bc_mid[64:96, :], bc_rest[64:96, :]).then_inc(mid_done, 1)

            def softplus_in(nb):
                act.wait_ge(z_done, nb)
                wait(act, delta_done, nb - 1)
                for dt in range(HC):
                    nc.scalar.activation(zabs[:, dt], bank_l[2 + dt][:], ACT.Abs, bias=bdt_sb[:, dt:dt + 1]).then_inc(z_taken, 1)
                    nc.scalar.activation(zpos[:, dt], bank_l[2 + dt][:], ACT.Relu, bias=bdt_sb[:, dt:dt + 1]).then_inc(z_taken, 1)
                act.wait_ge(z_taken, nb * 4)
                nc.scalar.activation(zabs[:], zabs[:], ACT.Exp, scale=-1.0).then_inc(sp_step, 1)

            def softplus_ln(nb):
                act.wait_ge(sp_step, nb * 2 - 1)
                nc.scalar.activation(zabs[:], zabs[:], ACT.Ln, bias=1.0).then_inc(sp_step, 1)

            def skip_term(par, loaded, used):
                act.wait_ge(xnt_in[par], loaded)
                wait(act, sum_done, used)
                for dt in range(HC):
                    i = nc.scalar.activation(skip[:, par, dt], xnt[:, par, dt], ACT.Copy, scale=dpar_sb[:, dt:dt + 1])
                i.then_inc(skip_done, 1)

            def decays(par, dpar_, sl, free, nb):
                act.wait_ge(delta_done, nb)
                wait(act, scan_done, free)
                for i in range(STEPS):
                    n = sl * STEPS + i
                    for dt in (1, 0):
                        nc.scalar.activation(decay[:, par, i, dt], delta[:, dpar_, dt], ACT.Exp,
                                             scale=a_sb[:, dt, n:n + 1]).then_inc(decay_done, 1)

            def take_ext(k, nu, used):
                act.wait_ge(ex_tr, nu)
                wait(act, up_done, used)
                nc.scalar.copy(ext[:, k % 2], bank_l[0][:].rearrange("p (c t) -> p c t", c=HC)).then_inc(ext_done, 1)

            for half in range(2):
                act.wait_ge(probs_tr, half + 1)
                nc.scalar.copy(work[:, half], bank_l[half][:]).then_inc(work_in, 1)
            act.wait_ge(a_made, 1)
            skip_term(0, 16, 0)
            take_bc(1)
            take_mid(1)
            softplus_in(1)
            softplus_ln(1)
            decays(0, 0, 0, 0, 1)
            act.wait_ge(picks_done, 4)
            act.wait_ge(b1_in, 32)
            act.wait_ge(b2_moved, 16 * 6)
            take_ext(0, 1, 0)

            def main(j):
                for k in range(BU):
                    m, sl = k // SLOTS, k % SLOTS
                    u, b = j * BU + k, j * BODY + m
                    e2 = k // 8
                    if k % 8 == 0 and there(u, NU):
                        wait(act, down_done, u - 8)
                        nc.scalar.copy(b1_st[:, e2], b1_all[:, :, :].rearrange("p a f -> p (a f)")[:, bass.ds(j * 2 * FC + e2 * FC, FC)]).then_inc(staged, 1)
                        nc.scalar.copy(b2_st[:, e2], b2_all[:, bass.ds(j * 2 * D + e2 * D, D)]).then_inc(staged, 1)
                    if sl == 0 and there(b, NB):
                        nc.scalar.copy(gate_st[:, m], gate_all[:, bass.ds(b * 8, 8)]).then_inc(gates_staged, 1)
                    if there(u - 2, NU):
                        act.wait_ge(down_done, u - 1)
                        wait(act, scattered, u * 32 - 96)
                        gm = ((k - 2) // SLOTS) % BODY
                        act.wait_ge(gates_staged, b + (1 if sl >= 2 else 0))
                        for i in range(UB):
                            col = 2 * ((sl + 2) % SLOTS) + i
                            nc.scalar.activation(og[:, k % 2, i], bank_o[:, i * D:(i + 1) * D], ACT.Copy,
                                                 scale=gate_st[:, gm, col:col + 1]).then_inc(og_done, 1)
                    if there(b, NB) and there(b + 1, NB):
                        if sl == 0:
                            par = (m + 1) % 2
                            skip_term(par, (j * 2 + (m + 1) // 2 + 1) * 16, b * N - N + 1)
                        if sl == 1:
                            take_bc(b + 2)
                        if sl == 2:
                            softplus_in(b + 2)
                    if sl == 3 and there(b - 1, NB):
                        act.wait_ge(y_tr, b)
                        wait(act, y_added, b * 16 - 16)
                        for i in range(2):
                            nc.scalar.copy(yrow[:, 2 * i:2 * i + 2], bank_l[2 + i][:].rearrange("p (c d) -> p c d", c=2)).then_inc(yrow_done, 1)
                    if there(u + 1, NU):
                        nd = ((k + 1) // SLOTS) % 2
                        decays((k + 1) % 2, nd, (sl + 1) % SLOTS, u * 8, b + (2 if sl == 3 else 1))
                    if there(b, NB) and there(b + 1, NB):
                        if sl == 1:
                            take_mid(b + 2)
                        if sl == 2:
                            softplus_ln(b + 2)
                    if there(u, NU):
                        act.wait_ge(staged, j * 4 + 2 * e2 + 2)
                        wait(act, down_done, u - 1)
                        for f in range(FC):
                            if f % 2 == 0:
                                act.wait_ge(up_done, u * 4 + f // 2 + 1)
                            nc.scalar.activation(hid[:, k % 2, f], bank_l[f // 2][:, (f % 2) * UT:(f % 2 + 1) * UT],
                                                 ACT.Gelu_apprx_tanh, bias=b1_st[:, e2, f:f + 1]).then_inc(gelu_done, 1)
                    if there(u + 1, NU):
                        take_ext(k + 1, u + 2, u * 4)

            both(main, NJ)(act)

        @block.vector
        def _(dve):
            nc.vector.memset(ones3[:], 1.0).then_inc(consts_set, 1)
            dve.wait_ge(row_made, 1)
            nc.vector.tensor_scalar(row_i[:, 1:2], row_i[:, 0:1], P - E, (T // E).bit_length() - 1, ALU.bitwise_and,
                                    ALU.logical_shift_left).then_inc(row_made, 1)
            dve.wait_ge(row_made, 2)
            nc.vector.tensor_copy(row_f[:, 0:1], row_i[:, 1:2]).then_inc(row_made, 1)
            dve.wait_ge(row_made, 3)
            nc.vector.tensor_scalar(row_f[:, 1:2], row_f[:, 0:1], float(HALF * T), None, ALU.add).then_inc(row_made, 1)
            dve.wait_ge(params_in, 16 * 7)
            nc.vector.tensor_copy(b2_hi[:], b2_f).then_inc(b2_step, 1)
            dve.wait_ge(b2_step, 1)
            nc.vector.tensor_tensor(b2_f, b2_f, b2_hi[:], ALU.subtract).then_inc(b2_step, 1)
            dve.wait_ge(b2_step, 2)
            nc.vector.tensor_copy(b2_mid[:], b2_f).then_inc(b2_step, 1)
            dve.wait_ge(b2_step, 3)
            nc.vector.tensor_tensor(b2_f, b2_f, b2_mid[:], ALU.subtract).then_inc(b2_step, 1)
            dve.wait_ge(b2_step, 4)
            nc.vector.tensor_copy(b2_lo[:], b2_f).then_inc(b2_step, 1)
            dve.wait_ge(a_exp, 1)
            nc.vector.tensor_scalar(a_sb[:], a_sb[:], -1.0, None, ALU.mult).then_inc(a_made, 1)

            def rows(q):
                for r in range(4):
                    b = q * 4 + r
                    if there(b, NB):
                        dve.wait_ge(x_in[r], q * 16 + 16)
                        for c in range(TC):
                            nc.vector.bn_stats(stats[:, r, c], xin[:, r, c]).then_inc(stats_done, 1)
                        dve.wait_ge(stats_done, b * TC + TC)
                        dve.sem_inc(turn["dve"], 1)
                        for c in range(TC):
                            nc.vector.bn_aggr(mv[:, r, c], stats[:, r, c]).then_inc(mv_done, 1)
                        dve.wait_ge(mv_done, b * TC + TC)
                        nc.vector.tensor_scalar(vare[:, r], mv[:, r, :, 1], EPS, None, ALU.add).then_inc(vare_done, 1)
                    if there(b - 1, NB):
                        g = (r - 1) % 4
                        dve.wait_ge(rstd_done, b)
                        wait(dve, rows_out[g], (q if r >= 1 else q - 1) * 16)
                        wait(dve, xn_tr, b - 4)
                        for c in range(TC):
                            i = nc.vector.tensor_scalar(xno[:, g, c], xin[:, g, c], mv[:, g, c, 0:1], rstd[:, g, c:c + 1],
                                                        ALU.subtract, ALU.mult)
                        i.then_inc(xn_done, 1)
                    if there(b - 3, NB):
                        g = (r - 3) % 4
                        par = (r - 3) % 2
                        lg = (bank_o, bank_c)[par][:, 0:TC * E].rearrange("p (c e) -> p c e", c=TC)
                        dve.wait_ge(logits_done, b - 2)
                        nc.vector.reduce_max(lmax[:, g], lg, axis=AX.X).then_inc(lmax_done, 1)
                        dve.wait_ge(lmax_done, b - 2)
                        nc.vector.tensor_tensor(lsh[:, g], lg, lmax[:, g].unsqueeze(2).broadcast_to([P, TC, E]),
                                                ALU.subtract).then_inc(lsh_done, 1)
                    if there(b - 4, NB):
                        g = r % 4
                        dve.wait_ge(lexp_done, b - 3)
                        nc.vector.reduce_sum(lsum[:, g], lexp[:, g], axis=AX.X).then_inc(lnorm, 1)
                        dve.wait_ge(lnorm, b * 2 - 7)
                        nc.vector.reciprocal(lrec[:, g], lsum[:, g]).then_inc(lnorm, 1)
                        dve.wait_ge(lnorm, b * 2 - 6)
                        nc.vector.tensor_tensor(probs[:, :, bass.ds(b - 4, 1), :].rearrange("p c b e -> p c (b e)"),
                                                lexp[:, g], lrec[:, g].unsqueeze(2).broadcast_to([P, TC, E]),
                                                ALU.mult).then_inc(probs_done, 1)

            both(rows, NB // 4)(dve)

            def take_rest(nb):
                dve.wait_ge(hi_done, nb)
                wait(dve, lo_done, nb - 1)
                nc.vector.tensor_tensor(bc_rest[64:96, :], bank_l[3][64:96, :], bc_hi[64:96, :],
                                        ALU.subtract).then_inc(rest_done, 1)

            def take_lo(nb, par, used):
                dve.wait_ge(mid_done, nb)
                wait(dve, c_ready, used)
                nc.vector.tensor_tensor(bcs[64:96, par], bc_rest[64:96, :], bc_mid[64:96, :],
                                        ALU.subtract).then_inc(lo_done, 1)

            def take_delta(nb, par, decays_done, loaded):
                dve.wait_ge(sp_step, nb * 2)
                wait(dve, decay_done, decays_done)
                nc.vector.tensor_tensor(delta[:, par], zpos[:], zabs[:], ALU.add).then_inc(delta_done, 1)
                dve.wait_ge(delta_done, nb)
                dve.wait_ge(xnt_in[par], loaded)
                nc.vector.tensor_tensor(du[:, par], delta[:, par], xnt[:, par], ALU.mult).then_inc(du_done, 1)

            take_rest(1)
            take_lo(1, 0, 0)
            ops = 0
            for half in range(2):
                dve.wait_ge(work_in, half + 1)
            for t in range(K // 8):
                for half in range(2):
                    v8, i8, w = vals[:, half, 8 * t:8 * t + 8], idx_u[:, half, 8 * t:8 * t + 8], work[:, half]
                    if t:
                        dve.wait_ge(round_op, 6 * t - 3 + 3 * half)
                    nc.vector.max(v8, w).then_inc(round_op, 1)
                    dve.wait_ge(round_op, 6 * t + 3 * half + 1)
                    nc.vector.max_index(i8, v8, w).then_inc(round_op, 1)
                    nc.vector.match_replace(w, v8, w, -1.0).then_inc(round_op, 1)
            dve.wait_ge(round_op, 6 * K // 8)
            dve.wait_ge(row_made, 4)
            for half in range(2):
                nc.vector.tensor_scalar(idx_f[:, half], idx_u[:, half], row_f[:, half:half + 1], None,
                                        ALU.add).then_inc(picks, 1)
            dve.wait_ge(picks_tr, 1)
            for half in range(2):
                for dst, part in ((idx_all, half), (gate_all, 2 + half)):
                    nc.vector.tensor_copy(dst[:, half * P:(half + 1) * P].rearrange("p (e b) -> p b e", e=E),
                                          bank_l[0][:, part * P:(part + 1) * P].rearrange("p (b e) -> p b e", e=E)
                                          ).then_inc(picks_done, 1)
            take_delta(1, 0, 0, 16)

            def main(j):
                for k in range(BU):
                    m, sl = k // SLOTS, k % SLOTS
                    u, b = j * BU + k, j * BODY + m
                    if not there(b, NB):
                        continue
                    par = m % 2
                    for i in range(STEPS):
                        n = sl * STEPS + i
                        s = b * N + n
                        dve.wait_ge(b_ready, s + 1)
                        dve.wait_ge(du_done, b + 1)
                        wait(dve, scan_done, s * 2)
                        nc.vector.tensor_tensor(bank_x[:], bank_b[:], du[:, par, 0], ALU.mult).then_inc(bx_done, 1)
                        nc.vector.tensor_tensor(bank_b[:], bank_b[:], du[:, par, 1], ALU.mult).then_inc(bx_done, 1)
                        wait(dve, prod_done, s * 2 - 2)
                        dve.wait_ge(decay_done, s * 2 + 1)
                        dve.wait_ge(bx_done, s * 2 + 2)
                        nc.vector.tensor_tensor_scan(state[:, i % 2, 1], decay[:, k % 2, i, 1], bank_b[:], 0.0,
                                                     ALU.mult, ALU.add).then_inc(scan_done, 1)
                        dve.wait_ge(decay_done, s * 2 + 2)
                        nc.vector.tensor_tensor_scan(state[:, i % 2, 0], decay[:, k % 2, i, 0], bank_x[:], 0.0,
                                                     ALU.mult, ALU.add).then_inc(scan_done, 1)
                        dve.wait_ge(c_ready, s + 1)
                        wait(dve, sum_done, s - 3)
                        dve.wait_ge(scan_done, s * 2 + 1)
                        nc.vector.tensor_tensor(prod[:, i, 1], state[:, i % 2, 1], bank_c[:], ALU.mult).then_inc(prod_done, 1)
                        dve.wait_ge(scan_done, s * 2 + 2)
                        nc.vector.tensor_tensor(prod[:, i, 0], state[:, i % 2, 0], bank_c[:], ALU.mult).then_inc(prod_done, 1)
                        if sl == 1 and i == 0 and there(b + 1, NB):
                            take_rest(b + 2)
                        if sl == 2 and i == 0 and there(b + 1, NB):
                            take_lo(b + 2, (m + 1) % 2, b * N)
                        if sl == 2 and i == 3 and there(b + 1, NB):
                            take_delta(b + 2, (m + 1) % 2, b * 2 * N, (j * 2 + (m + 1) // 2 + 1) * 16)

            both(main, NJ)(dve)

        @block.tensor
        def _(pe):
            pe.wait_ge(params_in, 16 * 7)
            pe.wait_ge(ident_made, 2)

            def rows(q):
                for r in range(4):
                    b = q * 4 + r
                    par = r % 2
                    if there(b, NB):
                        pe.wait_ge(xn_done, b + 1)
                        wait(pe, xnt_done, b * 2 - 2)
                        for hc in range(HC):
                            for c in range(TC):
                                i = nc.tensor.transpose(bank_l[2 * par + hc][:, c * P:(c + 1) * P],
                                                        xno[:, r, c, hc * P:(hc + 1) * P], ident[:])
                        i.then_inc(xn_tr, 1)
                    if there(b - 1, NB):
                        pp = (r - 1) % 2
                        lg = (bank_o, bank_c)[pp]
                        pe.wait_ge(xnt_done, b * 2)
                        wait(pe, lsh_done, b - 2)
                        for c in range(TC):
                            for hc in range(HC):
                                i = nc.tensor.matmul(lg[:, c * E:(c + 1) * E], xtr[:, pp, hc, c * P:(c + 1) * P],
                                                     wg_sb[:, hc], start=(hc == 0), stop=(hc == HC - 1))
                        i.then_inc(logits_done, 1)

            both(rows, NB // 4)(pe)

            def project(nb, par, loaded):
                pe.wait_ge(xnt_in[par], loaded)
                for hc in range(HC):
                    i = nc.tensor.matmul(bank_l[3][0:BC, :], wdbc_sb[:, hc], xnt[:, par, hc],
                                         start=(hc == 0), stop=(hc == HC - 1))
                i.then_inc(bc_proj, 1)

            def expand(nb):
                pe.wait_ge(low_done, nb)
                for dt in range(HC):
                    i = nc.tensor.matmul(bank_l[2 + dt][:], wdt_sb[:, dt * P:(dt + 1) * P], low[:], start=True, stop=True)
                i.then_inc(z_done, 1)

            def chosen_columns(k, count):
                pe.wait_ge(gathered[k % 2], count)
                for i in range(UB):
                    for hc in range(HC):
                        o = nc.tensor.transpose(bank_l[0][:, hc * UT + i * K:hc * UT + (i + 1) * K],
                                                ex[:, k % 2, i, hc * P:(hc + 1) * P], ident[:])
                o.then_inc(ex_tr, 1)

            def y_rows(par):
                for c in range(TC):
                    for dt in range(HC):
                        o = nc.tensor.transpose(bank_l[2 + c // 2][:, (c % 2) * D + dt * P:(c % 2) * D + (dt + 1) * P],
                                                ysum[:, par, dt, c * P:(c + 1) * P], ident[:])
                o.then_inc(y_tr, 1)

            pe.wait_ge(probs_done, NB)
            for half in range(2):
                for c in range(TC):
                    i = nc.tensor.transpose(bank_l[half][:, c * P:(c + 1) * P],
                                            probs[:, c, half * HALF:(half + 1) * HALF, :].rearrange("p b e -> p (b e)"), ident[:])
                i.then_inc(probs_tr, 1)
            project(1, 0, 16)
            pe.wait_ge(hi_done, 1)
            pe.wait_ge(rest_done, 1)
            expand(1)
            pe.wait_ge(picks, 2)
            pe.wait_ge(work_in, 2)
            for half in range(2):
                nc.tensor.transpose(bank_l[0][:, half * P:(half + 1) * P], idx_f[:, half], ident[:])
            for half in range(2):
                i = nc.tensor.transpose(bank_l[0][:, (2 + half) * P:(3 + half) * P], vals[:, half], ident[:])
            i.then_inc(picks_tr, 1)
            pe.wait_ge(picks_done, 4)
            chosen_columns(0, 32)
            pe.wait_ge(sel_made, 4)
            pe.wait_ge(consts_set, 2)

            def main(j):
                for k in range(BU):
                    m, sl = k // SLOTS, k % SLOTS
                    u, b = j * BU + k, j * BODY + m
                    e2, le2 = k // 8, ((k - 1) // 8) % 2
                    for q in range(2 * STEPS):
                        s = u * STEPS + q // 2
                        n = sl * STEPS + q // 2
                        if there(b, NB):
                            if q == 0 and sl == 0:
                                pe.wait_ge(hi_moved, b * 16 + 16)
                                pe.wait_ge(mid_moved, b * 16 + 16)
                                pe.wait_ge(lo_done, b + 1)
                            if q % 2 == 0:
                                wait(pe, scan_done, s * 2 - 1)
                                nc.tensor.matmul(bank_b[:], sel[:, n], bcs[:, m % 2], start=True, stop=True).then_inc(b_ready, 1)
                            else:
                                wait(pe, prod_done, s * 2)
                                nc.tensor.matmul(bank_c[:], sel[:, N + n], bcs[:, m % 2], start=True, stop=True).then_inc(c_ready, 1)
                        if q < 4 and there(u, NU):
                            if q == 0:
                                pe.wait_ge(ext_done, u + 1)
                                if k % 8 == 0:
                                    pe.wait_ge(w1_in[e2], j * 16 + 16)
                            else:
                                wait(pe, gelu_done, u * 8 - 8 + 2 * q + 2)
                            if there(b, NB) and there(b + 1, NB):
                                if q == 3 and sl == 1:
                                    pe.wait_ge(low_done, b + 2)
                                    pe.wait_ge(rest_done, b + 2)
                                if q == 2 and sl == 2:
                                    pe.wait_ge(z_taken, b * 4 + 6)
                                if q == 3 and sl == 2:
                                    pe.wait_ge(z_taken, b * 4 + 8)
                            if q >= 2 and sl == 3 and there(b - 1, NB):
                                pe.wait_ge(yrow_done, b * 2 + q - 3)
                            for f in (2 * q, 2 * q + 1):
                                for hc in range(HC):
                                    i = nc.tensor.matmul(bank_l[q][:, (f % 2) * UT:(f % 2 + 1) * UT],
                                                         w1_sb[:, e2, hc, f * P:(f + 1) * P], ext[:, k % 2, hc],
                                                         start=(hc == 0), stop=(hc == HC - 1))
                            i.then_inc(up_done, 1)
                        if q >= 4 and there(u - 1, NU):
                            if q == 4:
                                wait(pe, og_done, u * 2 - 2)
                                pe.wait_ge(gelu_done, u * 8)
                                if k % 8 == 1:
                                    pe.wait_ge(w2_in[e2], j * 16 + 16)
                                    pe.wait_ge(staged, j * 4 + 2 * e2 + 2)
                            c = (q - 4) // 2
                            o = bank_o[:, c * D:(c + 1) * D]
                            if q % 2 == 0:
                                nc.tensor.matmul(o, ones3[:], b2_st[:, le2], start=True, stop=False)
                            for f in range(4 * (q % 2), 4 * (q % 2) + 4):
                                i = nc.tensor.matmul(o, hid[:, (k - 1) % 2, f, c * K:(c + 1) * K], w2_sb[:, le2, f],
                                                     start=False, stop=(f == FC - 1))
                            if q == 7:
                                i.then_inc(down_done, 1)
                        if q == 5 and there(u + 1, NU):
                            pe.wait_ge(gelu_done, u * 8 + 2)
                            chosen_columns(k + 1, (j * 8 + (k + 1) // 2 + 1) * 32)
                    if there(u, NU) and there(b + 1, NB):
                        if sl == 0:
                            pe.wait_ge(gelu_done, u * 8 + 8)
                            project(b + 2, (m + 1) % 2, (j * 2 + (m + 1) // 2 + 1) * 16)
                        if sl == 1:
                            pe.wait_ge(gelu_done, u * 8 + 8)
                            expand(b + 2)
                    if sl == 2 and there(b - 1, NB):
                        if there(u, NU):
                            pe.wait_ge(gelu_done, u * 8 + 8)
                        pe.wait_ge(sum_done, b * N)
                        y_rows((m - 1) % 2)

            both(main, NJ)(pe)


_NAMES = ["x", "wdbc", "wdt", "bdt", "alog", "dpar", "wg", "w1", "b1", "w2", "b2"]


def kernel(**inputs):
    import concourse.bacc as _bacc
    from concourse.bass_utils import run_bass_kernel_spmd as _run

    g = {k: np.asarray(v) for k, v in inputs.items()}
    laid = {
        "x": g["L0_attn_x"],
        "wdbc": g["L0_attn_W_deltaBC"].T,
        "wdt": g["L0_attn_W_dt"].T,
        "bdt": g["L0_attn_b_dt"].reshape(HC, P).T,
        "alog": g["L0_attn_A_log"].reshape(HC, P, N).transpose(1, 0, 2),
        "dpar": g["L0_attn_D_param"].reshape(HC, P).T,
        "wg": g["L0_ffn_Wg"].T,
        "w1": g["L0_ffn_W1"],
        "b1": g["L0_ffn_b1"].reshape(E, FC, P).transpose(2, 0, 1).reshape(P, E * FC),
        "w2": g["L0_ffn_W2"],
        "b2": g["L0_ffn_b2"].reshape(1, E * D),
    }
    nc = _bacc.Bacc("TRN2", target_bir_lowering=False, num_devices=1)
    arrays, args = {}, []
    for name in _NAMES:
        a = np.ascontiguousarray(laid[name])
        arrays[f"in_{name}"] = a
        args.append(nc.dram_tensor(f"in_{name}", a.shape, mybir.dt.from_np(a.dtype), kind="ExternalInput").ap())
    out = nc.dram_tensor("out_0", (NB, T, D), F32, kind="ExternalOutput").ap()
    build(nc, *args, out)
    r = _run(nc, [arrays], core_ids=[0])
    return r.results[0]["out_0"]
```

```python
import numpy as np
import concourse.bass as bass
from concourse import mybir
from contextlib import ExitStack

F32 = mybir.dt.float32
BF16 = mybir.dt.bfloat16
F32R = mybir.dt.float32r
U32 = mybir.dt.uint32
I32 = mybir.dt.int32
ALU = mybir.AluOpType
ACT = mybir.ActivationFunctionType
AX = mybir.AxisListType

P = 128
NB, T, D = 32, 512, 256
R, N = 64, 16
E, K, F = 8, 128, 1024
TC, HC, FC = T // P, D // P, F // P
BC = R + 2 * N
HALF = NB // 2
UB = 2
UT = UB * K
SLOTS = 4
STEPS = N // SLOTS
BODY = 4
BU = BODY * SLOTS
NJ = NB // BODY
NU = NB * SLOTS
LATE = 6
W1_PARTS = 4
EPS = 1e-5


def wait(eng, sem, value):
    if not (isinstance(value, int) and value <= 0):
        eng.wait_ge(sem, value)


def there(index, count):
    return not isinstance(index, int) or 0 <= index < count


def build(nc, x, wdbc, wdt, bdt, alog, dpar, wg, w1, b1, w2, b2, out):
    ctx = ExitStack()
    with ctx:
        def sb(name, shape, dt=F32):
            return ctx.enter_context(nc.sbuf_tensor(name, shape, dt))

        def bank(name):
            return ctx.enter_context(nc.psum_tensor(name, [P, 512], F32))

        def sem(name):
            return ctx.enter_context(nc.semaphore(name))

        xn_rows = nc.dram_tensor("xn_rows", [NB * T, D], F32, kind="Internal").ap()
        xn_cols = nc.dram_tensor("xn_cols", [NB, P, HC, T], F32, kind="Internal").ap()
        x_tiles = x.rearrange("b (c p) d -> b p c d", p=P)
        out_rows = out.rearrange("b t d -> (b t) d")
        out_tiles = out.rearrange("b (c p) d -> b p c d", p=P)
        xn_tiles = xn_rows.rearrange("(b c p) d -> b p c d", p=P, c=TC)
        w1_tiles = w1.rearrange("e (c p) f -> e p c f", p=P)
        w2_tiles = w2.rearrange("e (c p) d -> e p c d", p=P)

        ident = sb("ident", [P, P])
        pick = sb("pick", [3 * 2 * N, 2 * N], BF16)
        ones3 = sb("ones3", [3, P], BF16)
        neg_half = sb("neg_half", [P, TC])
        wdbc_sb = sb("wdbc_sb", [P, HC, BC])
        wdt_sb = sb("wdt_sb", [R, D])
        bdt_sb = sb("bdt_sb", [P, HC])
        a_sb = sb("a_sb", [P, HC, N])
        dpar_sb = sb("dpar_sb", [P, HC])
        wg_sb = sb("wg_sb", [P, HC, E])
        b1_all = sb("b1_all", [P, 2, E * FC])
        b1_st = sb("b1_st", [P, 2, FC])
        b2_all = sb("b2_all", [3, E * D], BF16)
        b2_st = sb("b2_st", [3, 2, D], BF16)
        w1_raw = sb("w1_raw", [P, F])
        w1_hi = sb("w1_hi", [P, 2, HC, F], F32R)
        w1_lo = sb("w1_lo", [P, 2, HC, F], F32R)
        w2_sb = sb("w2_sb", [P, 2, FC, D])
        decay = sb("decay", [P, 2, STEPS, HC, T])
        xnt = sb("xnt", [P, 2, HC, T])
        delta = sb("delta", [P, 2, HC, T])
        du = sb("du", [P, 2, HC, T])
        skip = sb("skip", [P, HC, T])
        state = sb("state", [P, 2, HC, T])
        prod = sb("prod", [P, 4, HC, T])
        ysum = sb("ysum", [P, 2, HC, T])
        zabs = sb("zabs", [P, HC, T])
        yrow = sb("yrow", [P, TC, D])
        low = sb("low", [R, T])
        bc_hi = sb("bc_hi", [P, T], BF16)
        bc_mid = sb("bc_mid", [P, T], BF16)
        bc_rest = sb("bc_rest", [P, T])
        bcs = sb("bcs", [3 * 2 * N, 2, T], BF16)
        ex = sb("ex", [P, 2, UB, D])
        ext_hi = sb("ext_hi", [P, 2, HC, UT], F32R)
        ext_lo = sb("ext_lo", [P, 2, HC, UT], F32R)
        hid = sb("hid", [P, 2, FC, UT])
        og = sb("og", [P, 2, UB, D])
        idx_all = sb("idx_all", [P, 2 * P], U32)
        gate_all = sb("gate_all", [P, 2 * P])
        idx_st = sb("idx_st", [P, BODY, 8], U32)
        gate_st = sb("gate_st", [P, BODY, 8])
        dflat = decay[:, :, :, :, :].rearrange("p a b c t -> p (a b c t)")
        xin = dflat[:, 0:4 * 1024].rearrange("p (r c d) -> p r c d", r=4, c=TC)
        xno = dflat[:, 4 * 1024:8 * 1024].rearrange("p (r c d) -> p r c d", r=4, c=TC)
        xtr = delta[:, :, :, :]
        hflat = hid[:, :, :, :].rearrange("p a f t -> p (a f t)")
        at = [0]

        def small(*shape):
            n = int(np.prod(shape))
            at[0] += n
            t = hflat[:, at[0] - n:at[0]]
            return t.rearrange("p (a b) -> p a b", a=shape[0]) if len(shape) == 2 else t.rearrange(
                "p (a b c) -> p a b c", a=shape[0], b=shape[1])

        probs = small(TC, NB, E)
        stats, mv = small(4, TC, 6), small(4, TC, 2)
        lsh, lexp = small(4, TC, E), small(4, TC, E)
        vare, rstd, lmax, lsum, lrec = (small(4, TC) for _ in range(5))
        work = prod[:, 0, :, :]
        vals, idx_f = small(2, K), small(2, K)
        idx_u = small(2, K).bitcast(U32)
        row_i = sb("row_i", [P, 2], I32)
        row_f = sb("row_f", [P, 2])
        b2_f = prod[0:1, 1:3, :, :].rearrange("p a b t -> p (a b t)")
        b2_r = prod[0:1, 3:4, :, :]
        b2_hi = ysum[0:1, 0, :, :].rearrange("p c t -> p (c t)").bitcast(BF16)
        b2_mid = ysum[0:1, 1, :, :].rearrange("p c t -> p (c t)").bitcast(BF16)
        b2_lo = yrow[0:1, :, :].rearrange("p c t -> p (c t)").bitcast(BF16)

        bank_b, bank_o = bank("bank_b"), bank("bank_o")
        bank_c, bank_t = bank("bank_c"), bank("bank_t")
        bank_l = [bank(f"bank_l{i}") for i in range(4)]

        params_in = sem("params_in")
        b1_in = sem("b1_in")
        ident_made = sem("ident_made")
        pick_made = sem("pick_made")
        row_made = sem("row_made")
        consts_set = sem("consts_set")
        zero_set = sem("zero_set")
        a_exp = sem("a_exp")
        a_made = sem("a_made")
        b2_step = sem("b2_step")
        b2_moved = sem("b2_moved")
        x_in = [sem(f"x_in{i}") for i in range(4)]
        resid_out = [sem(f"resid_out{i}") for i in range(4)]
        rows_out = [sem(f"rows_out{i}") for i in range(4)]
        cols_out = [sem(f"cols_out{i}") for i in range(2)]
        stats_done = sem("stats_done")
        mv_done = sem("mv_done")
        vare_done = sem("vare_done")
        rstd_done = sem("rstd_done")
        xn_done = sem("xn_done")
        xn_tr = sem("xn_tr")
        xnt_done = sem("xnt_done")
        logits_done = sem("logits_done")
        lmax_done = sem("lmax_done")
        lsh_done = sem("lsh_done")
        lexp_done = sem("lexp_done")
        lnorm = sem("lnorm")
        probs_done = sem("probs_done")
        probs_tr = sem("probs_tr")
        work_in = sem("work_in")
        round_op = sem("round_op")
        picks = sem("picks")
        picks_tr = sem("picks_tr")
        picks_done = sem("picks_done")
        xnt_in = [sem(f"xnt_in{i}") for i in range(2)]
        bc_proj = sem("bc_proj")
        hi_done = sem("hi_done")
        low_done = sem("low_done")
        rest_done = sem("rest_done")
        mid_done = sem("mid_done")
        lo_done = sem("lo_done")
        hi_moved = sem("hi_moved")
        mid_moved = sem("mid_moved")
        z_done = sem("z_done")
        z_taken = sem("z_taken")
        sp_step = sem("sp_step")
        delta_done = sem("delta_done")
        du_done = sem("du_done")
        skip_done = sem("skip_done")
        decay_done = sem("decay_done")
        b_ready = sem("b_ready")
        c_ready = sem("c_ready")
        bx_done = sem("bx_done")
        scan_done = sem("scan_done")
        prod_done = sem("prod_done")
        sum_done = sem("sum_done")
        y_tr = sem("y_tr")
        yrow_done = sem("yrow_done")
        y_added = sem("y_added")
        w1_in = sem("w1_in")
        w1_hi_done = sem("w1_hi_done")
        w1_lo_done = sem("w1_lo_done")
        w2_in = [sem(f"w2_in{i}") for i in range(2)]
        staged = sem("staged")
        gates_staged = sem("gates_staged")
        idx_staged = sem("idx_staged")
        gathered = [sem(f"gathered{i}") for i in range(2)]
        ex_tr = sem("ex_tr")
        ext_hi_done = sem("ext_hi_done")
        ext_lo_done = sem("ext_lo_done")
        up_done = sem("up_done")
        gelu_done = sem("gelu_done")
        down_done = sem("down_done")
        og_done = sem("og_done")
        scattered = sem("scattered")
        turn = {name: sem(f"turn_{name}") for name in ("sp", "pool", "dve")}

        def both(emit, count):
            def run(eng):
                emit(0)
                with eng.Fori(1, count - 1) as i:
                    emit(i)
                emit(count - 1)
                emit(count)
            return run

        block = ctx.enter_context(nc.Block())

        @block.sync
        def _(sp):
            def held(sem, value):
                wait(sp, sem, value)
                if not isinstance(value, int):
                    sp.sem_inc(turn["sp"], 1)

            for dst, src in ((wdbc_sb[:], wdbc.rearrange("(c p) m -> p c m", p=P)), (wdt_sb[:], wdt),
                             (bdt_sb[:], bdt), (a_sb[:], alog), (dpar_sb[:], dpar),
                             (wg_sb[:], wg.rearrange("(c p) e -> p c e", p=P)), (b2_f, b2)):
                sp.dma_start(dst, src).then_inc(params_in, 16)
            for half in range(2):
                sp.dma_start(b1_all[:, half], b1).then_inc(b1_in, 16)

            def rows(q):
                for r in range(4):
                    b = q * 4 + r
                    if there(b, NB):
                        held(xn_done, q * 4 + r - 3)
                        held(resid_out[r], q * 16)
                        sp.dma_start(xin[:, r], x_tiles[b]).then_inc(x_in[r], 16)
                    r2 = (r - 2) % 4
                    if there(b - 2, NB):
                        held(x_in[r2], (q + (0 if r >= 2 else -1)) * 16 + 16)
                        sp.dma_start(out_tiles[b - 2], xin[:, r2]).then_inc(resid_out[r2], 16)

            both(rows, NB // 4)(sp)

            held(b2_step, 5)
            for row, part in enumerate((b2_hi, b2_mid, b2_lo)):
                sp.dma_start(b2_all[row:row + 1, :], part).then_inc(b2_moved, 16)

            def load_w1(e, hc, ge):
                held(w1_lo_done, ge * W1_PARTS + hc * (W1_PARTS // 2))
                sp.dma_start(w1_raw[:], w1_tiles[e][:, hc]).then_inc(w1_in, 16)

            def load_w2(e, par, free):
                held(down_done, free)
                sp.dma_start(w2_sb[:, par], w2_tiles[e]).then_inc(w2_in[par], 16)

            load_w1(0, 0, 0)
            load_w2(0, 0, 0)
            for r in range(4):
                held(resid_out[r], 16 * NB // 4)
                held(rows_out[r], 16 * NB // 4)
            for r in range(2):
                held(cols_out[r], 16 * NB // 2)
            for b in range(2):
                sp.dma_start(xnt[:, b], xn_cols[b]).then_inc(xnt_in[b], 16)

            def move_parts(nb, par, used):
                held(hi_done, nb)
                held(c_ready, used)
                sp.dma_start(bcs[0:32, par], bc_hi[64:96, :]).then_inc(hi_moved, 16)
                held(mid_done, nb)
                sp.dma_start(bcs[32:64, par], bc_mid[64:96, :]).then_inc(mid_moved, 16)

            move_parts(1, 0, 0)
            load_w1(0, 1, 0)

            def main(j):
                for m in range(BODY):
                    b = j * BODY + m
                    if not there(b, NB):
                        continue
                    if there(b + 2, NB):
                        held(du_done, b + 1)
                        held(skip_done, b + 1)
                        held(bc_proj, b + 1)
                        sp.dma_start(xnt[:, m % 2], xn_cols[b + 2]).then_inc(xnt_in[m % 2], 16)
                    if there(j * 2 + m // 2 + 1, NJ * 2):
                        load_w1((j * 2 + m // 2 + 1) % E, m % 2, j * 2 + m // 2 + 1)
                    if m == 0:
                        load_w2((j * 2 + 1) % E, 1, j * BU)
                    if m == 2 and there(j + 1, NJ):
                        load_w2((j * 2 + 2) % E, 0, j * BU + BU // 2)
                    if there(b + 1, NB):
                        move_parts(b + 2, (m + 1) % 2, b * N)

            both(main, NJ)(sp)
            held(y_added, 16 * NB)
            held(scattered, 32 * NU)

        @block.gpsimd
        def _(pool):
            nc.gpsimd.memset(ident[:], 0.0).then_inc(ident_made, 1)
            nc.gpsimd.memset(neg_half[:], -0.5).then_inc(consts_set, 1)
            pool.wait_ge(ident_made, 1)
            nc.gpsimd.affine_select(out=ident[:], in_=ident[:], compare_op=ALU.not_equal, fill=1.0, base=0,
                                    pattern=[[-1, P]], channel_multiplier=1).then_inc(ident_made, 1)
            nc.gpsimd.iota(row_i[:, 0:1], pattern=[[0, 1]], base=0, channel_multiplier=1).then_inc(row_made, 1)
            nc.gpsimd.memset(pick[:], 0.0).then_inc(pick_made, 1)
            for part in range(3):
                pool.wait_ge(pick_made, part + 1)
                nc.gpsimd.affine_select(out=pick[:], in_=pick[:], compare_op=ALU.not_equal, fill=1.0,
                                        base=-32 * part, pattern=[[-1, 2 * N]],
                                        channel_multiplier=1).then_inc(pick_made, 1)

            def rows(q):
                for r in range(4):
                    b = q * 4 + r
                    if there(b, NB):
                        pool.wait_ge(vare_done, b + 1)
                        nc.gpsimd.tensor_tensor(rstd[:, r], vare[:, r], neg_half[:], ALU.pow).then_inc(rstd_done, 1)
                    if there(b - 1, NB):
                        r1 = (r - 1) % 4
                        pool.wait_ge(xn_done, b)
                        pool.dma_start(xn_tiles[b - 1], xno[:, r1]).then_inc(rows_out[r1], 16)

            both(rows, NB // 4)(pool)
            for r in range(4):
                pool.wait_ge(resid_out[r], 16 * NB // 4)
                pool.wait_ge(rows_out[r], 16 * NB // 4)

            def stage_idx(m, col):
                nc.gpsimd.tensor_copy(idx_st[:, m], idx_all[:, bass.ds(col, 8)]).then_inc(idx_staged, 1)

            def gather(k, sl, m, passes, ga_free):
                wait(pool, ex_tr, ga_free)
                pool.wait_ge(idx_staged, passes)
                pool.sem_inc(turn["pool"], 1)
                for i in range(UB):
                    pool.indirect_dma_start(
                        out=ex[:, k % 2, i], out_offset=None, in_=xn_rows,
                        in_offset=bass.IndirectOffsetOnAxis(ap=idx_st[:, m, 2 * sl + i:2 * sl + i + 1], axis=0),
                    ).then_inc(gathered[k % 2], 16)

            pool.wait_ge(b2_moved, 16 * 3)
            pool.wait_ge(picks_done, 4)
            stage_idx(0, 0)
            gather(0, 0, 0, 1, 0)
            gather(1, 1, 0, 1, 0)

            def split_w1(ge, par, hc, piece):
                pool.wait_ge(w1_hi_done, ge * HC + hc + 1)
                w = F * HC // W1_PARTS
                cols = slice(piece * w, (piece + 1) * w)
                nc.gpsimd.tensor_tensor(w1_lo[:, par, hc, cols], w1_raw[:, cols], w1_hi[:, par, hc, cols].bitcast(F32),
                                        ALU.subtract).then_inc(w1_lo_done, 1)

            for hc in range(HC):
                for piece in range(W1_PARTS // HC):
                    split_w1(0, 0, hc, piece)

            def main(j):
                for k in range(BU):
                    m, sl = k // SLOTS, k % SLOTS
                    u, b = j * BU + k, j * BODY + m
                    for i in range(STEPS):
                        n = sl * STEPS + i
                        s = b * N + n
                        if there(b, NB):
                            pool.wait_ge(prod_done, s + 1)
                            if n == 0:
                                pool.wait_ge(skip_done, b + 1)
                                wait(pool, y_tr, b * 2 - 2)
                                first = skip[:]
                            else:
                                pool.wait_ge(sum_done, s)
                                first = ysum[:, m % 2]
                            nc.gpsimd.tensor_tensor(ysum[:, m % 2], first, prod[:, i], ALU.add).then_inc(sum_done, 1)
                        if i % 2 == 1 and sl == 2 and there(u, NU - BU // 2):
                            split_w1(j * 2 + k // 8 + 1, (k // 8 + 1) % 2, m % 2, i // 2)
                        if i == 0:
                            if sl == 2 and there(b + 1, NB):
                                wait(pool, scattered, u * 32 - 64 * 2)
                                stage_idx((m + 1) % BODY, b * 8 + 8)
                            if there(u + 2, NU):
                                nm = ((k + 2) // SLOTS) % BODY
                                gather(k, (sl + 2) % SLOTS, nm, b + (2 if sl >= 2 else 1), u + 1)
                        if i in (1, 2) and there(u - 2, NU):
                            c = i - 1
                            sm = ((k - 2) // SLOTS) % BODY
                            pool.wait_ge(og_done, u * 2 - 2)
                            wait(pool, scattered, u * 32 - 64 + 16 * c)
                            wait(pool, y_added, b * 16 - (32 if sl == 0 else 16))
                            so = 2 * ((sl + 2) % SLOTS) + c
                            pool.sem_inc(turn["pool"], 1)
                            pool.indirect_dma_start(
                                out=out_rows,
                                out_offset=bass.IndirectOffsetOnAxis(ap=idx_st[:, sm, so:so + 1], axis=0),
                                in_=og[:, k % 2, c], in_offset=None, compute_op=ALU.add,
                            ).then_inc(scattered, 16)
                        if i == 3 and sl == 0 and there(b - 2, NB):
                            pool.wait_ge(yrow_done, b * 2 - 2)
                            if isinstance(u, int):
                                pool.wait_ge(scattered, 32 * min(u - 1, NU))
                            else:
                                pool.wait_ge(scattered, u * 32 - 32)
                            pool.dma_start(out_tiles[b - 2], yrow[:], accum_op=ALU.add).then_inc(y_added, 16)

            both(main, NJ)(pool)

        @block.scalar
        def _(act):
            act.wait_ge(params_in, 16 * 7)
            nc.scalar.activation(a_sb[:], a_sb[:], ACT.Exp).then_inc(a_exp, 1)

            def rows(q):
                for r in range(4):
                    b = q * 4 + r
                    par = r % 2
                    if there(b - 3, NB):
                        act.wait_ge(lsh_done, b - 2)
                        nc.scalar.activation(lexp[:, (r - 3) % 4], lsh[:, (r - 3) % 4], ACT.Exp).then_inc(lexp_done, 1)
                    if there(b, NB):
                        act.wait_ge(xn_tr, b + 1)
                        wait(act, cols_out[par], (q * 2 + r // 2) * 16)
                        wait(act, logits_done, b - 1)
                        for hc in range(HC):
                            nc.scalar.copy(xtr[:, par, hc], bank_l[2 * par + hc][:]).then_inc(xnt_done, 1)
                        act.wait_ge(xnt_done, b * 2 + 2)
                        act.dma_start(xn_cols[b], xtr[:, par]).then_inc(cols_out[par], 16)

            both(rows, NB // 4)(act)

            def take_bc(nb):
                act.wait_ge(bc_proj, nb)
                wait(act, hi_moved, nb * 16 - 16)
                nc.scalar.copy(bc_hi[64:96, :], bank_t[64:96, :]).then_inc(hi_done, 1)
                wait(act, z_done, nb * 2 - 2)
                nc.scalar.copy(low[:], bank_t[0:R, :]).then_inc(low_done, 1)

            def take_yrow(half, taken, added):
                act.wait_ge(y_tr, taken)
                wait(act, y_added, added)
                nc.scalar.copy(yrow[:, 2 * half:2 * half + 2], bank_t[:].rearrange("p (c d) -> p c d", c=2)).then_inc(yrow_done, 1)

            def take_mid(nb):
                act.wait_ge(rest_done, nb)
                wait(act, mid_moved, nb * 16 - 16)
                wait(act, lo_done, nb - 1)
                nc.scalar.copy(bc_mid[64:96, :], bc_rest[64:96, :]).then_inc(mid_done, 1)

            def take_z(nb, par, dt):
                act.wait_ge(z_done, nb * 2 - 1 + dt)
                wait(act, delta_done, nb - 1)
                wait(act, du_done, nb - 2)
                wait(act, decay_done, (nb - 2) * 2 * N)
                nc.scalar.activation(zabs[:, dt], bank_t[:], ACT.Abs, bias=bdt_sb[:, dt:dt + 1]).then_inc(z_taken, 1)
                nc.scalar.activation(delta[:, par, dt], bank_t[:], ACT.Relu, bias=bdt_sb[:, dt:dt + 1]).then_inc(z_taken, 1)

            def softplus_exp(nb):
                act.wait_ge(z_taken, nb * 4)
                nc.scalar.activation(zabs[:], zabs[:], ACT.Exp, scale=-1.0).then_inc(sp_step, 1)

            def softplus_ln(nb):
                act.wait_ge(sp_step, nb * 2 - 1)
                nc.scalar.activation(zabs[:], zabs[:], ACT.Ln, bias=1.0).then_inc(sp_step, 1)

            def skip_term(par, loaded, used):
                act.wait_ge(xnt_in[par], loaded)
                wait(act, sum_done, used)
                for dt in range(HC):
                    i = nc.scalar.activation(skip[:, dt], xnt[:, par, dt], ACT.Copy, scale=dpar_sb[:, dt:dt + 1])
                i.then_inc(skip_done, 1)

            def decays(par, dpar_, sl, free, nb):
                act.wait_ge(delta_done, nb)
                wait(act, scan_done, free)
                for i in range(STEPS):
                    n = sl * STEPS + i
                    for dt in range(HC):
                        nc.scalar.activation(decay[:, par, i, dt, 1:T], delta[:, dpar_, dt, 1:T], ACT.Exp,
                                             scale=a_sb[:, dt, n:n + 1]).then_inc(decay_done, 1)

            def take_ext(k, nu, used):
                act.wait_ge(ex_tr, nu)
                wait(act, up_done, used)
                nc.scalar.copy(ext_hi[:, k % 2], bank_t[:].rearrange("p (c t) -> p c t", c=HC)).then_inc(ext_hi_done, 1)

            def round_w1(ge, par, hc, used):
                act.wait_ge(w1_in, (ge * HC + hc) * 16 + 16)
                wait(act, up_done, used)
                nc.scalar.copy(w1_hi[:, par, hc], w1_raw[:]).then_inc(w1_hi_done, 1)

            for half in range(2):
                act.wait_ge(probs_tr, half + 1)
                nc.scalar.copy(work[:, half], bank_l[half][:]).then_inc(work_in, 1)
            act.wait_ge(a_made, 1)
            for par in range(2):
                act.wait_ge(cols_out[par], 16 * NB // 2)
            act.wait_ge(logits_done, NB)
            skip_term(0, 16, 0)
            take_bc(1)
            take_mid(1)
            for dt in range(HC):
                take_z(1, 0, dt)
            softplus_exp(1)
            softplus_ln(1)
            act.wait_ge(zero_set, 1)
            decays(0, 0, 0, 0, 1)
            act.wait_ge(picks_done, 4)
            act.wait_ge(b1_in, 32)
            act.wait_ge(b2_moved, 16 * 3)
            round_w1(0, 0, 0, 0)
            round_w1(0, 0, 1, 0)
            take_ext(0, 1, 0)

            def main(j):
                for k in range(BU):
                    m, sl = k // SLOTS, k % SLOTS
                    u, b = j * BU + k, j * BODY + m
                    e2 = k // 8
                    if k % 8 == 0 and there(u, NU):
                        wait(act, down_done, u - 8)
                        nc.scalar.copy(b1_st[:, e2], b1_all[:, :, :].rearrange("p a f -> p (a f)")[:, bass.ds(j * 2 * FC + e2 * FC, FC)]).then_inc(staged, 1)
                        nc.scalar.copy(b2_st[:, e2], b2_all[:, bass.ds((j * 2 + e2) % E * D, D)]).then_inc(staged, 1)
                    if sl == 0 and there(b, NB):
                        nc.scalar.copy(gate_st[:, m], gate_all[:, bass.ds(b * 8, 8)]).then_inc(gates_staged, 1)
                    if there(u - 2, NU):
                        act.wait_ge(down_done, u - 1)
                        wait(act, scattered, u * 32 - 96)
                        gm = ((k - 2) // SLOTS) % BODY
                        act.wait_ge(gates_staged, b + (1 if sl >= 2 else 0))
                        for i in range(UB):
                            col = 2 * ((sl + 2) % SLOTS) + i
                            nc.scalar.activation(og[:, k % 2, i], bank_o[:, i * D:(i + 1) * D], ACT.Copy,
                                                 scale=gate_st[:, gm, col:col + 1]).then_inc(og_done, 1)
                    if there(b, NB) and there(b + 1, NB):
                        if sl == 3:
                            skip_term((m + 1) % 2, (j * 2 + (m + 1) // 2 + 1) * 16, b * N + 1)
                        if sl == 2:
                            take_z(b + 2, (m + 1) % 2, 1)
                            softplus_exp(b + 2)
                    if sl == 3 and there(b - 1, NB):
                        take_yrow(0, b * 2 - 1, b * 16 - 16)
                    if there(u + 1, NU):
                        nd = ((k + 1) // SLOTS) % 2
                        decays((k + 1) % 2, nd, (sl + 1) % SLOTS, u * 4, b + (2 if sl == 3 else 1))
                        take_ext(k + 1, u + 2, u * 4)
                    if there(b, NB) and there(b + 1, NB):
                        if sl == 1:
                            take_mid(b + 2)
                        if sl == 2:
                            softplus_ln(b + 2)
                    if sl == 0 and there(u, NU - BU // 2):
                        round_w1(j * 2 + e2 + 1, (e2 + 1) % 2, m % 2, (u - k % 8) * 4)
                    if there(u, NU):
                        act.wait_ge(staged, j * 4 + 2 * e2 + 2)
                        wait(act, down_done, u - 1)
                        for f in range(FC):
                            if f % 2 == 0:
                                act.wait_ge(up_done, u * 4 + f // 2 + 1)
                            nc.scalar.activation(hid[:, k % 2, f], bank_l[f // 2][:, (f % 2) * UT:(f % 2 + 1) * UT],
                                                 ACT.Gelu_apprx_tanh, bias=b1_st[:, e2, f:f + 1]).then_inc(gelu_done, 1)
                    if there(b, NB) and there(b + 1, NB):
                        if sl == 0:
                            take_bc(b + 2)
                        if sl == 1:
                            take_z(b + 2, (m + 1) % 2, 0)
                    if sl == 3 and there(b - 1, NB):
                        take_yrow(1, b * 2, b * 16 - 16)

            both(main, NJ)(act)

        @block.vector
        def _(dve):
            nc.vector.memset(ones3[:], 1.0).then_inc(consts_set, 1)
            dve.wait_ge(row_made, 1)
            nc.vector.tensor_scalar(row_i[:, 1:2], row_i[:, 0:1], P - E, (T // E).bit_length() - 1, ALU.bitwise_and,
                                    ALU.logical_shift_left).then_inc(row_made, 1)
            dve.wait_ge(row_made, 2)
            nc.vector.tensor_copy(row_f[:, 0:1], row_i[:, 1:2]).then_inc(row_made, 1)
            dve.wait_ge(row_made, 3)
            nc.vector.tensor_scalar(row_f[:, 1:2], row_f[:, 0:1], float(HALF * T), None, ALU.add).then_inc(row_made, 1)
            dve.wait_ge(params_in, 16 * 7)
            nc.vector.tensor_copy(b2_hi[:], b2_f).then_inc(b2_step, 1)
            dve.wait_ge(b2_step, 1)
            nc.vector.tensor_tensor(b2_f, b2_f, b2_hi[:], ALU.subtract).then_inc(b2_step, 1)
            dve.wait_ge(b2_step, 2)
            nc.vector.tensor_copy(b2_mid[:], b2_f).then_inc(b2_step, 1)
            dve.wait_ge(b2_step, 3)
            nc.vector.tensor_tensor(b2_f, b2_f, b2_mid[:], ALU.subtract).then_inc(b2_step, 1)
            dve.wait_ge(b2_step, 4)
            nc.vector.tensor_copy(b2_lo[:], b2_f).then_inc(b2_step, 1)
            dve.wait_ge(a_exp, 1)
            nc.vector.tensor_scalar(a_sb[:], a_sb[:], -1.0, None, ALU.mult).then_inc(a_made, 1)

            def rows(q):
                for r in range(4):
                    b = q * 4 + r
                    if there(b, NB):
                        dve.wait_ge(x_in[r], q * 16 + 16)
                        for c in range(TC):
                            nc.vector.bn_stats(stats[:, r, c], xin[:, r, c]).then_inc(stats_done, 1)
                        dve.wait_ge(stats_done, b * TC + TC)
                        dve.sem_inc(turn["dve"], 1)
                        for c in range(TC):
                            nc.vector.bn_aggr(mv[:, r, c], stats[:, r, c]).then_inc(mv_done, 1)
                        dve.wait_ge(mv_done, b * TC + TC)
                        nc.vector.tensor_scalar(vare[:, r], mv[:, r, :, 1], EPS, None, ALU.add).then_inc(vare_done, 1)
                    if there(b - 1, NB):
                        g = (r - 1) % 4
                        dve.wait_ge(rstd_done, b)
                        wait(dve, rows_out[g], (q if r >= 1 else q - 1) * 16)
                        wait(dve, xn_tr, b - 4)
                        for c in range(TC):
                            i = nc.vector.tensor_scalar(xno[:, g, c], xin[:, g, c], mv[:, g, c, 0:1], rstd[:, g, c:c + 1],
                                                        ALU.subtract, ALU.mult)
                        i.then_inc(xn_done, 1)
                    if there(b - 3, NB):
                        g = (r - 3) % 4
                        par = (r - 3) % 2
                        lg = (bank_o, bank_c)[par][:, 0:TC * E].rearrange("p (c e) -> p c e", c=TC)
                        dve.wait_ge(logits_done, b - 2)
                        nc.vector.reduce_max(lmax[:, g], lg, axis=AX.X).then_inc(lmax_done, 1)
                        dve.wait_ge(lmax_done, b - 2)
                        nc.vector.tensor_tensor(lsh[:, g], lg, lmax[:, g].unsqueeze(2).broadcast_to([P, TC, E]),
                                                ALU.subtract).then_inc(lsh_done, 1)
                    if there(b - 4, NB):
                        g = r % 4
                        dve.wait_ge(lexp_done, b - 3)
                        nc.vector.reduce_sum(lsum[:, g], lexp[:, g], axis=AX.X).then_inc(lnorm, 1)
                        dve.wait_ge(lnorm, b * 2 - 7)
                        nc.vector.reciprocal(lrec[:, g], lsum[:, g]).then_inc(lnorm, 1)
                        dve.wait_ge(lnorm, b * 2 - 6)
                        nc.vector.tensor_tensor(probs[:, :, bass.ds(b - 4, 1), :].rearrange("p c b e -> p c (b e)"),
                                                lexp[:, g], lrec[:, g].unsqueeze(2).broadcast_to([P, TC, E]),
                                                ALU.mult).then_inc(probs_done, 1)

            both(rows, NB // 4)(dve)

            def take_rest(nb):
                dve.wait_ge(hi_done, nb)
                wait(dve, lo_done, nb - 1)
                nc.vector.tensor_tensor(bc_rest[64:96, :], bank_t[64:96, :], bc_hi[64:96, :],
                                        ALU.subtract).then_inc(rest_done, 1)

            def take_lo(nb, par, used):
                dve.wait_ge(mid_done, nb)
                wait(dve, c_ready, used)
                nc.vector.tensor_tensor(bcs[64:96, par], bc_rest[64:96, :], bc_mid[64:96, :],
                                        ALU.subtract).then_inc(lo_done, 1)

            def ext_low(k, nu, used):
                dve.wait_ge(ext_hi_done, nu)
                wait(dve, up_done, used)
                nc.vector.tensor_tensor(ext_lo[:, k % 2], bank_t[:].rearrange("p (c t) -> p c t", c=HC),
                                        ext_hi[:, k % 2].bitcast(F32), ALU.subtract).then_inc(ext_lo_done, 1)

            def take_delta(nb, par):
                dve.wait_ge(sp_step, nb * 2)
                nc.vector.tensor_tensor(delta[:, par], delta[:, par], zabs[:], ALU.add).then_inc(delta_done, 1)

            def take_du(nb, par, loaded):
                dve.wait_ge(delta_done, nb)
                dve.wait_ge(xnt_in[par], loaded)
                nc.vector.tensor_tensor(du[:, par], delta[:, par], xnt[:, par], ALU.mult).then_inc(du_done, 1)

            take_rest(1)
            take_lo(1, 0, 0)
            def multiply_b(s, place, par, b):
                dve.wait_ge(b_ready, s + 1)
                dve.wait_ge(du_done, b + 1)
                wait(dve, prod_done, s - 1)
                nc.vector.tensor_tensor(state[:, place], du[:, par], bank_b[:][:, None, :].broadcast_to([P, HC, T]),
                                        ALU.mult).then_inc(bx_done, 1)

            ops = 0
            for half in range(2):
                dve.wait_ge(work_in, half + 1)
            for t in range(K // 8):
                for half in range(2):
                    v8, i8, w = vals[:, half, 8 * t:8 * t + 8], idx_u[:, half, 8 * t:8 * t + 8], work[:, half]
                    if t:
                        dve.wait_ge(round_op, 6 * t - 3 + 3 * half)
                    nc.vector.max(v8, w).then_inc(round_op, 1)
                    dve.wait_ge(round_op, 6 * t + 3 * half + 1)
                    nc.vector.max_index(i8, v8, w).then_inc(round_op, 1)
                    nc.vector.match_replace(w, v8, w, -1.0).then_inc(round_op, 1)
            dve.wait_ge(round_op, 6 * K // 8)
            dve.wait_ge(row_made, 4)
            for half in range(2):
                nc.vector.tensor_scalar(idx_f[:, half], idx_u[:, half], row_f[:, half:half + 1], None,
                                        ALU.add).then_inc(picks, 1)
            dve.wait_ge(picks_tr, 1)
            for half in range(2):
                for dst, part in ((idx_all, half), (gate_all, 2 + half)):
                    nc.vector.tensor_copy(dst[:, half * P:(half + 1) * P].rearrange("p (e b) -> p b e", e=E),
                                          bank_l[0][:, part * P:(part + 1) * P].rearrange("p (b e) -> p b e", e=E)
                                          ).then_inc(picks_done, 1)
            for r in range(4):
                dve.wait_ge(resid_out[r], 16 * NB // 4)
                dve.wait_ge(rows_out[r], 16 * NB // 4)
            dve.wait_ge(xn_tr, NB)
            nc.vector.memset(decay[:, :, :, :, 0:1], 0.0).then_inc(zero_set, 1)
            take_delta(1, 0)
            take_du(1, 0, 16)
            ext_low(0, 1, 0)
            multiply_b(0, 0, 0, 0)

            def main(j):
                for k in range(BU):
                    m, sl = k // SLOTS, k % SLOTS
                    u, b = j * BU + k, j * BODY + m
                    if not there(b, NB):
                        continue
                    par = m % 2
                    for i in range(STEPS):
                        n = sl * STEPS + i
                        s = b * N + n
                        if sl == 1 and i == 0 and there(b + 1, NB):
                            take_rest(b + 2)
                        dve.wait_ge(decay_done, s * 2 + 2)
                        dve.wait_ge(bx_done, s + 1)
                        h = state[:, i % 2].rearrange("p c t -> p (c t)")
                        nc.vector.tensor_tensor_scan(h, decay[:, k % 2, i].rearrange("p c t -> p (c t)"), h, 0.0,
                                                     ALU.mult, ALU.add).then_inc(scan_done, 1)
                        if there(s + 1, NB * N):
                            multiply_b(s + 1, (i + 1) % 2, par if n < N - 1 else 1 - par, b if n < N - 1 else b + 1)
                        dve.wait_ge(c_ready, s + 1)
                        wait(dve, sum_done, s - 3)
                        dve.wait_ge(scan_done, s + 1)
                        nc.vector.tensor_tensor(prod[:, i], state[:, i % 2], bank_c[:][:, None, :].broadcast_to([P, HC, T]),
                                                ALU.mult).then_inc(prod_done, 1)
                        if i == 2 and there(u + 1, NU):
                            ext_low(k + 1, u + 2, u * 4)
                        if sl == 1 and i == 3 and there(b + 1, NB):
                            take_lo(b + 2, (m + 1) % 2, b * N)
                        if sl == 2 and i == 3 and there(b + 1, NB):
                            take_delta(b + 2, (m + 1) % 2)
                        if sl == 3 and i == 0 and there(b + 1, NB):
                            take_du(b + 2, (m + 1) % 2, (j * 2 + (m + 1) // 2 + 1) * 16)

            both(main, NJ)(dve)

        @block.tensor
        def _(pe):
            pe.wait_ge(params_in, 16 * 7)
            pe.wait_ge(ident_made, 2)

            def rows(q):
                for r in range(4):
                    b = q * 4 + r
                    par = r % 2
                    if there(b, NB):
                        pe.wait_ge(xn_done, b + 1)
                        wait(pe, xnt_done, b * 2 - 2)
                        for hc in range(HC):
                            for c in range(TC):
                                i = nc.tensor.transpose(bank_l[2 * par + hc][:, c * P:(c + 1) * P],
                                                        xno[:, r, c, hc * P:(hc + 1) * P], ident[:])
                        i.then_inc(xn_tr, 1)
                    if there(b - 1, NB):
                        pp = (r - 1) % 2
                        lg = (bank_o, bank_c)[pp]
                        pe.wait_ge(xnt_done, b * 2)
                        wait(pe, lsh_done, b - 2)
                        for c in range(TC):
                            for hc in range(HC):
                                i = nc.tensor.matmul(lg[:, c * E:(c + 1) * E], xtr[:, pp, hc, c * P:(c + 1) * P],
                                                     wg_sb[:, hc], start=(hc == 0), stop=(hc == HC - 1))
                        i.then_inc(logits_done, 1)

            both(rows, NB // 4)(pe)

            def project(nb, par, loaded):
                pe.wait_ge(xnt_in[par], loaded)
                for hc in range(HC):
                    i = nc.tensor.matmul(bank_t[0:BC, :], wdbc_sb[:, hc], xnt[:, par, hc],
                                         start=(hc == 0), stop=(hc == HC - 1))
                i.then_inc(bc_proj, 1)

            def expand(nb, dt):
                pe.wait_ge(low_done, nb)
                nc.tensor.matmul(bank_t[:], wdt_sb[:, dt * P:(dt + 1) * P], low[:], start=True, stop=True).then_inc(z_done, 1)

            def chosen_columns(k, count, taken):
                pe.wait_ge(gathered[k % 2], count)
                wait(pe, ext_lo_done, taken)
                for i in range(UB):
                    for hc in range(HC):
                        o = nc.tensor.transpose(bank_t[:, hc * UT + i * K:hc * UT + (i + 1) * K],
                                                ex[:, k % 2, i, hc * P:(hc + 1) * P], ident[:])
                o.then_inc(ex_tr, 1)

            def y_rows(par, half):
                for c in (2 * half, 2 * half + 1):
                    for dt in range(HC):
                        o = nc.tensor.transpose(bank_t[:, (c % 2) * D + dt * P:(c % 2) * D + (dt + 1) * P],
                                                ysum[:, par, dt, c * P:(c + 1) * P], ident[:])
                o.then_inc(y_tr, 1)

            pe.wait_ge(probs_done, NB)
            for half in range(2):
                for c in range(TC):
                    i = nc.tensor.transpose(bank_l[half][:, c * P:(c + 1) * P],
                                            probs[:, c, half * HALF:(half + 1) * HALF, :].rearrange("p b e -> p (b e)"), ident[:])
                i.then_inc(probs_tr, 1)
            project(1, 0, 16)
            pe.wait_ge(hi_done, 1)
            pe.wait_ge(rest_done, 1)
            expand(1, 0)
            pe.wait_ge(z_taken, 2)
            expand(1, 1)
            pe.wait_ge(picks, 2)
            pe.wait_ge(work_in, 2)
            for half in range(2):
                nc.tensor.transpose(bank_l[0][:, half * P:(half + 1) * P], idx_f[:, half], ident[:])
            for half in range(2):
                i = nc.tensor.transpose(bank_l[0][:, (2 + half) * P:(3 + half) * P], vals[:, half], ident[:])
            i.then_inc(picks_tr, 1)
            pe.wait_ge(picks_done, 4)
            pe.wait_ge(z_taken, 4)
            chosen_columns(0, 32, 0)
            pe.wait_ge(pick_made, 4)
            pe.wait_ge(consts_set, 2)

            def spread_b(s, n, par):
                wait(pe, bx_done, s)
                nc.tensor.matmul(bank_b[:], pick[:, n:n + 1].broadcast_to([3 * 2 * N, P]), bcs[:, par],
                                 start=True, stop=True).then_inc(b_ready, 1)

            def stack_whole(b):
                pe.wait_ge(hi_moved, b * 16 + 16)
                pe.wait_ge(mid_moved, b * 16 + 16)
                pe.wait_ge(lo_done, b + 1)

            stack_whole(0)
            spread_b(0, 0, 0)

            def main(j):
                for k in range(BU):
                    m, sl = k // SLOTS, k % SLOTS
                    u, b = j * BU + k, j * BODY + m
                    e2, le2 = k // 8, ((k - 1) // 8) % 2
                    for q in range(2 * STEPS):
                        s = u * STEPS + q // 2
                        n = sl * STEPS + q // 2
                        if there(b, NB):
                            if q % 2 == 0 and there(s + 1, NB * N):
                                if n == N - 1:
                                    stack_whole(b + 1)
                                spread_b(s + 1, (n + 1) % N, m % 2 if n < N - 1 else (m + 1) % 2)
                            if q % 2 == 1:
                                wait(pe, prod_done, s)
                                nc.tensor.matmul(bank_c[:], pick[:, N + n:N + n + 1].broadcast_to([3 * 2 * N, P]),
                                                 bcs[:, m % 2], start=True, stop=True).then_inc(c_ready, 1)
                        if q == 0 and sl == 2 and there(b, NB) and there(b + 1, NB):
                            pe.wait_ge(z_taken, b * 4 + 6)
                            expand(b + 2, 1)
                        if q == 0 and sl == 3 and there(b - 1, NB):
                            pe.wait_ge(sum_done, b * N)
                            y_rows((m - 1) % 2, 0)
                        if q == 2 and there(u + 1, NU):
                            if sl == 1 and there(b + 1, NB):
                                pe.wait_ge(low_done, b + 2)
                                pe.wait_ge(rest_done, b + 2)
                            if sl == 2 and there(b + 1, NB):
                                pe.wait_ge(z_taken, b * 4 + 8)
                            if sl == 3 and there(b - 1, NB):
                                pe.wait_ge(yrow_done, b * 2 - 1)
                            if sl == 0 and there(b - 2, NB):
                                pe.wait_ge(yrow_done, b * 2 - 2)
                            chosen_columns(k + 1, (j * 8 + (k + 1) // 2 + 1) * 32, u + 1)
                        if q < 4 and there(u, NU):
                            if q == 0:
                                pe.wait_ge(ext_lo_done, u + 1)
                                if k % 8 == 0:
                                    pe.wait_ge(w1_lo_done, (j * 2 + e2 + 1) * W1_PARTS)
                            wait(pe, gelu_done, u * 8 - 8 + 2 * q + 2)
                            for f in (2 * q, 2 * q + 1):
                                for hc in range(HC):
                                    for w, m_ in ((w1_hi, ext_hi), (w1_hi, ext_lo), (w1_lo, ext_hi)):
                                        i = nc.tensor.matmul(bank_l[q][:, (f % 2) * UT:(f % 2 + 1) * UT],
                                                             w[:, e2, hc, f * P:(f + 1) * P], m_[:, k % 2, hc],
                                                             start=(hc == 0 and w is w1_hi and m_ is ext_hi),
                                                             stop=(hc == HC - 1 and w is w1_lo))
                            i.then_inc(up_done, 1)
                        if q >= 4 and there(u - 1, NU):
                            if q == 4:
                                wait(pe, og_done, u * 2 - 2)
                                pe.wait_ge(gelu_done, u * 8)
                                if k % 8 == 1:
                                    pe.wait_ge(w2_in[e2], j * 16 + 16)
                                    pe.wait_ge(staged, j * 4 + 2 * e2 + 2)
                            c = (q - 4) // 2
                            o = bank_o[:, c * D:(c + 1) * D]
                            if q % 2 == 0:
                                nc.tensor.matmul(o, ones3[:], b2_st[:, le2], start=True, stop=False)
                            for f in range(4 * (q % 2), 4 * (q % 2) + 4):
                                i = nc.tensor.matmul(o, hid[:, (k - 1) % 2, f, c * K:(c + 1) * K], w2_sb[:, le2, f],
                                                     start=False, stop=(f == FC - 1))
                            if q == 7:
                                i.then_inc(down_done, 1)
                        if q == LATE:
                            if there(u + 1, NU):
                                pe.wait_ge(ext_lo_done, u + 2)
                            if there(u, NU) and there(b + 1, NB):
                                if sl == 0:
                                    project(b + 2, (m + 1) % 2, (j * 2 + (m + 1) // 2 + 1) * 16)
                                if sl == 1:
                                    expand(b + 2, 0)
                            if sl == 3 and there(b - 1, NB):
                                if not there(u + 1, NU):
                                    pe.wait_ge(yrow_done, b * 2 - 1)
                                y_rows((m - 1) % 2, 1)

            both(main, NJ)(pe)


_NAMES = ["x", "wdbc", "wdt", "bdt", "alog", "dpar", "wg", "w1", "b1", "w2", "b2"]


def kernel(**inputs):
    import concourse.bacc as _bacc
    from concourse.bass_utils import run_bass_kernel_spmd as _run

    g = {k: np.asarray(v) for k, v in inputs.items()}
    laid = {
        "x": g["L0_attn_x"],
        "wdbc": g["L0_attn_W_deltaBC"].T,
        "wdt": g["L0_attn_W_dt"].T,
        "bdt": g["L0_attn_b_dt"].reshape(HC, P).T,
        "alog": g["L0_attn_A_log"].reshape(HC, P, N).transpose(1, 0, 2),
        "dpar": g["L0_attn_D_param"].reshape(HC, P).T,
        "wg": g["L0_ffn_Wg"].T,
        "w1": g["L0_ffn_W1"],
        "b1": g["L0_ffn_b1"].reshape(E, FC, P).transpose(2, 0, 1).reshape(P, E * FC),
        "w2": g["L0_ffn_W2"],
        "b2": g["L0_ffn_b2"].reshape(1, E * D),
    }
    nc = _bacc.Bacc("TRN2", target_bir_lowering=False, num_devices=1)
    arrays, args = {}, []
    for name in _NAMES:
        a = np.ascontiguousarray(laid[name])
        arrays[f"in_{name}"] = a
        args.append(nc.dram_tensor(f"in_{name}", a.shape, mybir.dt.from_np(a.dtype), kind="ExternalInput").ap())
    out = nc.dram_tensor("out_0", (NB, T, D), F32, kind="ExternalOutput").ap()
    build(nc, *args, out)
    r = _run(nc, [arrays], core_ids=[0])
    return r.results[0]["out_0"]
```

```python
import numpy as np
import concourse.bass as bass
from concourse import mybir
from contextlib import ExitStack

F32 = mybir.dt.float32
BF16 = mybir.dt.bfloat16
F32R = mybir.dt.float32r
U32 = mybir.dt.uint32
I32 = mybir.dt.int32
ALU = mybir.AluOpType
ACT = mybir.ActivationFunctionType
AX = mybir.AxisListType

P = 128
NB, T, D = 32, 512, 256
R, N = 64, 16
E, K, F = 8, 128, 1024
TC, HC, FC = T // P, D // P, F // P
BC = R + 2 * N
HALF = NB // 2
UB = 2
UT = UB * K
SLOTS = 4
STEPS = N // SLOTS
BODY = 4
BU = BODY * SLOTS
NJ = NB // BODY
NU = NB * SLOTS
LATE = 6
LEAD = 5
W1_PARTS = 4
EPS = 1e-5
GATE = 4
ROWS = 2 * GATE


def wait(eng, sem, value):
    if not (isinstance(value, int) and value <= 0):
        eng.wait_ge(sem, value)


def there(index, count):
    return not isinstance(index, int) or 0 <= index < count


def build(nc, x, wdbc, wdt, bdt, alog, dpar, wg, w1, b1, w2, b2, out):
    ctx = ExitStack()
    with ctx:
        def sb(name, shape, dt=F32):
            return ctx.enter_context(nc.sbuf_tensor(name, shape, dt))

        def bank(name):
            return ctx.enter_context(nc.psum_tensor(name, [P, 512], F32))

        def sem(name):
            return ctx.enter_context(nc.semaphore(name))

        xn_rows = nc.dram_tensor("xn_rows", [NB * T, D], F32, kind="Internal").ap()
        xn_cols = nc.dram_tensor("xn_cols", [NB, P, HC, T], F32, kind="Internal").ap()
        x_tiles = x.rearrange("b (c p) d -> b p c d", p=P)
        out_rows = out.rearrange("b t d -> (b t) d")
        out_tiles = out.rearrange("b (c p) d -> b p c d", p=P)
        xn_tiles = xn_rows.rearrange("(b c p) d -> b p c d", p=P, c=TC)
        w1_tiles = w1.rearrange("e (c p) f -> e p c f", p=P)
        w2_tiles = w2.rearrange("e (c p) d -> e p c d", p=P)

        ident = sb("ident", [P, P])
        pick = sb("pick", [3 * 2 * N, 2 * N], BF16)
        ones3 = sb("ones3", [3, P], BF16)
        neg_half = sb("neg_half", [P, TC])
        wdbc_sb = sb("wdbc_sb", [P, HC, BC])
        wdt_sb = sb("wdt_sb", [R, D])
        bdt_sb = sb("bdt_sb", [P, HC])
        a_sb = sb("a_sb", [P, HC, N])
        dpar_sb = sb("dpar_sb", [P, HC])
        wg_sb = sb("wg_sb", [P, HC, E])
        b1_all = sb("b1_all", [P, 2, E * FC])
        b1_st = sb("b1_st", [P, 2, FC])
        b2_all = sb("b2_all", [3, E * D], BF16)
        b2_st = sb("b2_st", [3, 2, D], BF16)
        w1_raw = sb("w1_raw", [P, F])
        w1_hi = sb("w1_hi", [P, 2, HC, F], F32R)
        w1_lo = sb("w1_lo", [P, 2, HC, F], F32R)
        w2_sb = sb("w2_sb", [P, 2, FC, D])
        decay = sb("decay", [P, 2, STEPS, HC, T])
        xnt = sb("xnt", [P, 2, HC, T])
        delta = sb("delta", [P, 2, HC, T])
        du = sb("du", [P, 2, HC, T])
        skip = sb("skip", [P, HC, T])
        state = sb("state", [P, 2, HC, T])
        prod = sb("prod", [P, 4, HC, T])
        ysum = sb("ysum", [P, 2, HC, T])
        zabs = sb("zabs", [P, HC, T])
        yrow = sb("yrow", [P, TC, D])
        low = sb("low", [R, T])
        bc_hi = sb("bc_hi", [P, T], BF16)
        bc_mid = sb("bc_mid", [P, T], BF16)
        bc_rest = sb("bc_rest", [P, T])
        bcs = sb("bcs", [3 * 2 * N, 2, T], BF16)
        ex = sb("ex", [P, 2, UB, D])
        ext_hi = sb("ext_hi", [P, 2, HC, UT], F32R)
        ext_lo = sb("ext_lo", [P, 2, HC, UT], F32R)
        hid = sb("hid", [P, 2, FC, UT])
        og = sb("og", [P, 2, UB, D])
        idx_all = sb("idx_all", [P, 2 * P], U32)
        gate_all = sb("gate_all", [P, 2 * P])
        idx_st = sb("idx_st", [P, BODY, 8], U32)
        gate_st = sb("gate_st", [P, BODY, 8])
        dflat = decay[:, :, :, :, :].rearrange("p a b c t -> p (a b c t)")
        xin = dflat[:, 0:4 * 1024].rearrange("p (r c d) -> p r c d", r=4, c=TC)
        xno = dflat[:, 4 * 1024:8 * 1024].rearrange("p (r c d) -> p r c d", r=4, c=TC)
        xtr = delta[:, :, :, :]
        hflat = hid[:, :, :, :].rearrange("p a f t -> p (a f t)")
        at = [0]

        def small(*shape):
            n = int(np.prod(shape))
            at[0] += n
            t = hflat[:, at[0] - n:at[0]]
            return t.rearrange("p (a b) -> p a b", a=shape[0]) if len(shape) == 2 else t.rearrange(
                "p (a b c) -> p a b c", a=shape[0], b=shape[1])

        probs = small(TC, NB, E)
        stats, mv = small(4, TC, 6), small(4, TC, 2)
        lsh, lexp = small(2, TC * GATE, E), small(2, TC * GATE, E)
        vare, rstd, shift = (small(4, TC) for _ in range(3))
        lmax, lsum, lrec = (small(2, TC * GATE) for _ in range(3))
        wg_wide = small(HC * GATE, GATE * E)
        lgt = small(1, T)[0:GATE * E, 0]
        work = prod[:, 0, :, :]
        vals, idx_f = small(2, K), small(2, K)
        idx_u = small(2, K).bitcast(U32)
        row_i = sb("row_i", [P, 2], I32)
        row_f = sb("row_f", [P, 2])
        b2_f = prod[0:1, 1:3, :, :].rearrange("p a b t -> p (a b t)")
        b2_r = prod[0:1, 3:4, :, :]
        b2_hi = ysum[0:1, 0, :, :].rearrange("p c t -> p (c t)").bitcast(BF16)
        b2_mid = ysum[0:1, 1, :, :].rearrange("p c t -> p (c t)").bitcast(BF16)
        b2_lo = yrow[0:1, :, :].rearrange("p c t -> p (c t)").bitcast(BF16)

        bank_b, bank_o = bank("bank_b"), bank("bank_o")
        bank_c, bank_t = bank("bank_c"), bank("bank_t")
        bank_l = [bank(f"bank_l{i}") for i in range(4)]

        params_in = sem("params_in")
        b1_in = sem("b1_in")
        ident_made = sem("ident_made")
        pick_made = sem("pick_made")
        row_made = sem("row_made")
        consts_set = sem("consts_set")
        zero_set = sem("zero_set")
        wide_set = sem("wide_set")
        a_exp = sem("a_exp")
        a_made = sem("a_made")
        b2_step = sem("b2_step")
        b2_moved = sem("b2_moved")
        x_in = [sem(f"x_in{i}") for i in range(4)]
        resid_out = [sem(f"resid_out{i}") for i in range(2)]
        rows_out = [sem(f"rows_out{i}") for i in range(4)]
        cols_out = [sem(f"cols_out{i}") for i in range(2)]
        stats_done = sem("stats_done")
        mv_done = sem("mv_done")
        vare_done = sem("vare_done")
        rstd_done = sem("rstd_done")
        shift_done = sem("shift_done")
        xn_done = sem("xn_done")
        xn_tr = sem("xn_tr")
        xnt_done = sem("xnt_done")
        logits_done = sem("logits_done")
        lgt_done = sem("lgt_done")
        lg_tr = sem("lg_tr")
        lmax_done = sem("lmax_done")
        lsh_done = sem("lsh_done")
        lexp_done = sem("lexp_done")
        lnorm = sem("lnorm")
        probs_done = sem("probs_done")
        probs_tr = sem("probs_tr")
        work_in = sem("work_in")
        round_op = sem("round_op")
        picks = sem("picks")
        picks_tr = sem("picks_tr")
        picks_done = sem("picks_done")
        xnt_in = [sem(f"xnt_in{i}") for i in range(2)]
        bc_proj = sem("bc_proj")
        hi_done = sem("hi_done")
        low_done = sem("low_done")
        rest_done = sem("rest_done")
        mid_done = sem("mid_done")
        lo_done = sem("lo_done")
        hi_moved = sem("hi_moved")
        mid_moved = sem("mid_moved")
        z_done = sem("z_done")
        z_taken = sem("z_taken")
        sp_step = sem("sp_step")
        delta_done = sem("delta_done")
        du_done = sem("du_done")
        skip_done = sem("skip_done")
        decay_done = sem("decay_done")
        b_ready = sem("b_ready")
        c_ready = sem("c_ready")
        bx_done = sem("bx_done")
        scan_done = sem("scan_done")
        prod_done = sem("prod_done")
        sum_done = sem("sum_done")
        y_tr = sem("y_tr")
        yrow_done = sem("yrow_done")
        y_added = sem("y_added")
        w1_in = sem("w1_in")
        w1_hi_done = sem("w1_hi_done")
        w1_lo_done = sem("w1_lo_done")
        w2_in = [sem(f"w2_in{i}") for i in range(2)]
        staged = sem("staged")
        gates_staged = sem("gates_staged")
        idx_staged = sem("idx_staged")
        gathered = [sem(f"gathered{i}") for i in range(2)]
        ex_tr = sem("ex_tr")
        ext_hi_done = sem("ext_hi_done")
        ext_lo_done = sem("ext_lo_done")
        up_done = sem("up_done")
        gelu_done = sem("gelu_done")
        down_done = sem("down_done")
        og_done = sem("og_done")
        scattered = sem("scattered")
        turn = {name: sem(f"turn_{name}") for name in ("sp", "pool", "dve", "pe")}

        def both(emit, count):
            def run(eng):
                emit(0)
                with eng.Fori(1, count - 1) as i:
                    emit(i)
                emit(count - 1)
                emit(count)
            return run

        block = ctx.enter_context(nc.Block())

        @block.sync
        def _(sp):
            def held(sem, value):
                wait(sp, sem, value)
                if not isinstance(value, int):
                    sp.sem_inc(turn["sp"], 1)

            for dst, src in ((wdbc_sb[:], wdbc.rearrange("(c p) m -> p c m", p=P)), (wdt_sb[:], wdt),
                             (bdt_sb[:], bdt), (a_sb[:], alog), (dpar_sb[:], dpar),
                             (wg_sb[:], wg.rearrange("(c p) e -> p c e", p=P)), (b2_f, b2)):
                sp.dma_start(dst, src).then_inc(params_in, 16)
            for half in range(2):
                sp.dma_start(b1_all[:, half], b1).then_inc(b1_in, 16)

            def rows(q):
                for r in range(ROWS):
                    b = q * ROWS + r
                    if there(b, NB):
                        held(xn_done, q * ROWS + r - 3)
                        sp.dma_start(xin[:, r % 4], x_tiles[b]).then_inc(x_in[r % 4], 16)
                    if there(b - 4, NB):
                        held(xnt_done, b * 2 - 6)
                        sp.dma_start(xn_cols[b - 4], xtr[:, r % 2]).then_inc(cols_out[r % 2], 16)

            both(rows, NB // ROWS)(sp)

            held(b2_step, 5)
            for row, part in enumerate((b2_hi, b2_mid, b2_lo)):
                sp.dma_start(b2_all[row:row + 1, :], part).then_inc(b2_moved, 16)

            def load_w1(e, hc, ge):
                held(w1_lo_done, ge * W1_PARTS + hc * (W1_PARTS // 2))
                sp.dma_start(w1_raw[:], w1_tiles[e][:, hc]).then_inc(w1_in, 16)

            def load_w2(e, par, free):
                held(down_done, free)
                sp.dma_start(w2_sb[:, par], w2_tiles[e]).then_inc(w2_in[par], 16)

            load_w1(0, 0, 0)
            load_w2(0, 0, 0)
            for r in range(4):
                held(rows_out[r], 16 * NB // 4)
            for r in range(2):
                held(cols_out[r], 16 * NB // 2)
            for b in range(2):
                sp.dma_start(xnt[:, b], xn_cols[b]).then_inc(xnt_in[b], 16)
            for half in range(2):
                sp.dma_start(out[half * HALF:(half + 1) * HALF], x[half * HALF:(half + 1) * HALF]).then_inc(resid_out[half], 16)

            def move_parts(nb, par, used):
                held(hi_done, nb)
                held(c_ready, used)
                sp.dma_start(bcs[0:32, par], bc_hi[64:96, :]).then_inc(hi_moved, 16)
                held(mid_done, nb)
                sp.dma_start(bcs[32:64, par], bc_mid[64:96, :]).then_inc(mid_moved, 16)

            move_parts(1, 0, 0)
            load_w1(0, 1, 0)

            def main(j):
                for m in range(BODY):
                    b = j * BODY + m
                    if not there(b, NB):
                        continue
                    if there(b + 2, NB):
                        held(du_done, b + 1)
                        held(skip_done, b + 1)
                        held(bc_proj, b + 1)
                        sp.dma_start(xnt[:, m % 2], xn_cols[b + 2]).then_inc(xnt_in[m % 2], 16)
                    if there(j * 2 + m // 2 + 1, NJ * 2):
                        load_w1((j * 2 + m // 2 + 1) % E, m % 2, j * 2 + m // 2 + 1)
                    if m == 0:
                        load_w2((j * 2 + 1) % E, 1, j * BU)
                    if m == 2 and there(j + 1, NJ):
                        load_w2((j * 2 + 2) % E, 0, j * BU + BU // 2)
                    if there(b + 1, NB):
                        move_parts(b + 2, (m + 1) % 2, b * N)

            both(main, NJ)(sp)
            held(y_added, 16 * NB)
            held(scattered, 32 * NU)

        @block.gpsimd
        def _(pool):
            nc.gpsimd.memset(ident[:], 0.0).then_inc(ident_made, 1)
            nc.gpsimd.memset(neg_half[:], -0.5).then_inc(consts_set, 1)
            pool.wait_ge(ident_made, 1)
            nc.gpsimd.affine_select(out=ident[:], in_=ident[:], compare_op=ALU.not_equal, fill=1.0, base=0,
                                    pattern=[[-1, P]], channel_multiplier=1).then_inc(ident_made, 1)
            nc.gpsimd.iota(row_i[:, 0:1], pattern=[[0, 1]], base=0, channel_multiplier=1).then_inc(row_made, 1)
            nc.gpsimd.memset(pick[:], 0.0).then_inc(pick_made, 1)
            for part in range(3):
                pool.wait_ge(pick_made, part + 1)
                nc.gpsimd.affine_select(out=pick[:], in_=pick[:], compare_op=ALU.not_equal, fill=1.0,
                                        base=-32 * part, pattern=[[-1, 2 * N]],
                                        channel_multiplier=1).then_inc(pick_made, 1)

            def rows(q):
                for r in range(ROWS):
                    b = q * ROWS + r
                    if there(b, NB):
                        pool.wait_ge(vare_done, b + 1)
                        wait(pool, xn_done, b - 3)
                        nc.gpsimd.tensor_tensor(rstd[:, r % 4], vare[:, r % 4], neg_half[:], ALU.pow).then_inc(rstd_done, 1)
                    if there(b - 2, NB):
                        pool.wait_ge(xn_done, b - 1)
                        pool.dma_start(xn_tiles[b - 2], xno[:, (r - 2) % 4]).then_inc(rows_out[(r - 2) % 4], 16)

            both(rows, NB // ROWS)(pool)
            pool.wait_ge(resid_out[0], 16)
            for r in range(4):
                pool.wait_ge(rows_out[r], 16 * NB // 4)

            def stage_idx(m, col):
                nc.gpsimd.tensor_copy(idx_st[:, m], idx_all[:, bass.ds(col, 8)]).then_inc(idx_staged, 1)

            def gather(k, sl, m, passes, ga_free):
                wait(pool, ex_tr, ga_free)
                pool.wait_ge(idx_staged, passes)
                pool.sem_inc(turn["pool"], 1)
                for i in range(UB):
                    pool.indirect_dma_start(
                        out=ex[:, k % 2, i], out_offset=None, in_=xn_rows,
                        in_offset=bass.IndirectOffsetOnAxis(ap=idx_st[:, m, 2 * sl + i:2 * sl + i + 1], axis=0),
                    ).then_inc(gathered[k % 2], 16)

            pool.wait_ge(b2_moved, 16 * 3)
            def split_w1(ge, par, hc, piece):
                pool.wait_ge(w1_hi_done, ge * HC + hc + 1)
                w = F * HC // W1_PARTS
                cols = slice(piece * w, (piece + 1) * w)
                nc.gpsimd.tensor_tensor(w1_lo[:, par, hc, cols], w1_raw[:, cols], w1_hi[:, par, hc, cols].bitcast(F32),
                                        ALU.subtract).then_inc(w1_lo_done, 1)

            for hc in range(HC):
                for piece in range(W1_PARTS // HC):
                    split_w1(0, 0, hc, piece)
            pool.wait_ge(picks_done, 2)
            stage_idx(0, 0)
            gather(0, 0, 0, 1, 0)
            gather(1, 1, 0, 1, 0)

            def main(j):
                for k in range(BU):
                    m, sl = k // SLOTS, k % SLOTS
                    u, b = j * BU + k, j * BODY + m
                    if isinstance(j, int) and j == 0 and k == BU - 1:
                        pool.wait_ge(resid_out[1], 16)
                    for i in range(STEPS):
                        n = sl * STEPS + i
                        s = b * N + n
                        if there(b, NB):
                            pool.wait_ge(prod_done, s + 1)
                            if n == 0:
                                pool.wait_ge(skip_done, b + 1)
                                wait(pool, y_tr, b * 2 - 2)
                                first = skip[:]
                            else:
                                pool.wait_ge(sum_done, s)
                                first = ysum[:, m % 2]
                            nc.gpsimd.tensor_tensor(ysum[:, m % 2], first, prod[:, i], ALU.add).then_inc(sum_done, 1)
                        if i % 2 == 1 and sl == 2 and there(u, NU - BU // 2):
                            split_w1(j * 2 + k // 8 + 1, (k // 8 + 1) % 2, m % 2, i // 2)
                        if i == 0:
                            if sl == 2 and there(b + 1, NB):
                                wait(pool, scattered, u * 32 - 64 * 2)
                                stage_idx((m + 1) % BODY, b * 8 + 8)
                            if there(u + 2, NU):
                                nm = ((k + 2) // SLOTS) % BODY
                                gather(k, (sl + 2) % SLOTS, nm, b + (2 if sl >= 2 else 1), u + 1)
                        if i in (1, 2) and there(u - 2, NU):
                            c = i - 1
                            sm = ((k - 2) // SLOTS) % BODY
                            pool.wait_ge(og_done, u * 2 - 2)
                            wait(pool, scattered, u * 32 - 64 + 16 * c)
                            wait(pool, y_added, b * 16 - (32 if sl == 0 else 16))
                            so = 2 * ((sl + 2) % SLOTS) + c
                            pool.sem_inc(turn["pool"], 1)
                            pool.indirect_dma_start(
                                out=out_rows,
                                out_offset=bass.IndirectOffsetOnAxis(ap=idx_st[:, sm, so:so + 1], axis=0),
                                in_=og[:, k % 2, c], in_offset=None, compute_op=ALU.add,
                            ).then_inc(scattered, 16)
                        if i == 3 and sl == 0 and there(b - 2, NB):
                            pool.wait_ge(yrow_done, b * 2 - 2)
                            if isinstance(u, int):
                                pool.wait_ge(scattered, 32 * min(u - 1, NU))
                            else:
                                pool.wait_ge(scattered, u * 32 - 32)
                            pool.dma_start(out_tiles[b - 2], yrow[:], accum_op=ALU.add).then_inc(y_added, 16)

            both(main, NJ)(pool)

        @block.scalar
        def _(act):
            act.wait_ge(params_in, 16 * 7)
            nc.scalar.activation(a_sb[:], a_sb[:], ACT.Exp).then_inc(a_exp, 1)

            def rows(q):
                for r in range(ROWS):
                    b = q * ROWS + r
                    g, gq = q * 2 + r // GATE, r // GATE % 2
                    if there(b - 1, NB):
                        i4 = (r - 1) % 4
                        act.wait_ge(shift_done, b)
                        wait(act, rows_out[i4], (q * 2 + (r - 1) // 4) * 16)
                        wait(act, xn_tr, b - 4)
                        for c in range(TC):
                            i = nc.scalar.activation(xno[:, i4, c], xin[:, i4, c], ACT.Identity,
                                                     bias=shift[:, i4, c:c + 1], scale=rstd[:, i4, c:c + 1])
                        i.then_inc(xn_done, 1)
                    if there(b - 2, NB):
                        par = r % 2
                        act.wait_ge(xn_tr, b - 1)
                        wait(act, cols_out[par], (q * (ROWS // 2) + (r - 2) // 2) * 16)
                        wait(act, logits_done, b - 3)
                        for hc in range(HC):
                            nc.scalar.copy(xtr[:, par, hc], bank_l[2 * par + hc][:]).then_inc(xnt_done, 1)
                    if r % GATE == 1 and there(g - 2, NB // GATE):
                        act.wait_ge(lsh_done, g - 1)
                        nc.scalar.activation(lexp[:, gq], lsh[:, gq], ACT.Exp).then_inc(lexp_done, 1)

            both(rows, NB // ROWS)(act)

            def take_bc(nb):
                act.wait_ge(bc_proj, nb)
                wait(act, hi_moved, nb * 16 - 16)
                nc.scalar.copy(bc_hi[64:96, :], bank_t[64:96, :]).then_inc(hi_done, 1)
                wait(act, z_done, nb * 2 - 2)
                nc.scalar.copy(low[:], bank_t[0:R, :]).then_inc(low_done, 1)

            def take_yrow(half, taken, added):
                act.wait_ge(y_tr, taken)
                wait(act, y_added, added)
                nc.scalar.copy(yrow[:, 2 * half:2 * half + 2], bank_t[:].rearrange("p (c d) -> p c d", c=2)).then_inc(yrow_done, 1)

            def take_mid(nb):
                act.wait_ge(rest_done, nb)
                wait(act, mid_moved, nb * 16 - 16)
                wait(act, lo_done, nb - 1)
                nc.scalar.copy(bc_mid[64:96, :], bc_rest[64:96, :]).then_inc(mid_done, 1)

            def take_z(nb, par, dt):
                act.wait_ge(z_done, nb * 2 - 1 + dt)
                wait(act, delta_done, nb - 1)
                wait(act, du_done, nb - 2)
                wait(act, decay_done, (nb - 2) * 2 * N)
                nc.scalar.activation(zabs[:, dt], bank_t[:], ACT.Abs, bias=bdt_sb[:, dt:dt + 1]).then_inc(z_taken, 1)
                nc.scalar.activation(delta[:, par, dt], bank_t[:], ACT.Relu, bias=bdt_sb[:, dt:dt + 1]).then_inc(z_taken, 1)

            def softplus_exp(nb):
                act.wait_ge(z_taken, nb * 4)
                nc.scalar.activation(zabs[:], zabs[:], ACT.Exp, scale=-1.0).then_inc(sp_step, 1)

            def softplus_ln(nb):
                act.wait_ge(sp_step, nb * 2 - 1)
                nc.scalar.activation(zabs[:], zabs[:], ACT.Ln, bias=1.0).then_inc(sp_step, 1)

            def skip_term(par, loaded, used):
                act.wait_ge(xnt_in[par], loaded)
                wait(act, sum_done, used)
                for dt in range(HC):
                    i = nc.scalar.activation(skip[:, dt], xnt[:, par, dt], ACT.Copy, scale=dpar_sb[:, dt:dt + 1])
                i.then_inc(skip_done, 1)

            def decays(par, dpar_, sl, free, nb):
                act.wait_ge(delta_done, nb)
                wait(act, scan_done, free)
                for i in range(STEPS):
                    n = sl * STEPS + i
                    for dt in range(HC):
                        nc.scalar.activation(decay[:, par, i, dt, 1:T], delta[:, dpar_, dt, 1:T], ACT.Exp,
                                             scale=a_sb[:, dt, n:n + 1]).then_inc(decay_done, 1)

            def take_ext(k, nu, used):
                act.wait_ge(ex_tr, nu)
                wait(act, up_done, used)
                nc.scalar.copy(ext_hi[:, k % 2], bank_t[:].rearrange("p (c t) -> p c t", c=HC)).then_inc(ext_hi_done, 1)

            def round_w1(ge, par, hc, used):
                act.wait_ge(w1_in, (ge * HC + hc) * 16 + 16)
                wait(act, up_done, used)
                nc.scalar.copy(w1_hi[:, par, hc], w1_raw[:]).then_inc(w1_hi_done, 1)

            for half in range(2):
                act.wait_ge(probs_tr, half + 1)
                nc.scalar.copy(work[:, half], bank_l[half][:]).then_inc(work_in, 1)
            act.wait_ge(a_made, 1)
            for par in range(2):
                act.wait_ge(cols_out[par], 16 * NB // 2)
            act.wait_ge(logits_done, NB)
            skip_term(0, 16, 0)
            take_bc(1)
            take_mid(1)
            for dt in range(HC):
                take_z(1, 0, dt)
            softplus_exp(1)
            softplus_ln(1)
            act.wait_ge(zero_set, 1)
            decays(0, 0, 0, 0, 1)
            round_w1(0, 0, 0, 0)
            round_w1(0, 0, 1, 0)
            act.wait_ge(b1_in, 32)
            act.wait_ge(b2_moved, 16 * 3)
            act.wait_ge(picks_done, 2)
            take_ext(0, 1, 0)

            def main(j):
                for k in range(BU):
                    m, sl = k // SLOTS, k % SLOTS
                    u, b = j * BU + k, j * BODY + m
                    e2 = k // 8
                    if k % 8 == 0 and there(u, NU):
                        wait(act, down_done, u - 8)
                        nc.scalar.copy(b1_st[:, e2], b1_all[:, :, :].rearrange("p a f -> p (a f)")[:, bass.ds(j * 2 * FC + e2 * FC, FC)]).then_inc(staged, 1)
                        nc.scalar.copy(b2_st[:, e2], b2_all[:, bass.ds((j * 2 + e2) % E * D, D)]).then_inc(staged, 1)
                    if sl == 0 and there(b, NB):
                        nc.scalar.copy(gate_st[:, m], gate_all[:, bass.ds(b * 8, 8)]).then_inc(gates_staged, 1)
                    if there(u - 2, NU):
                        act.wait_ge(down_done, u - 1)
                        wait(act, scattered, u * 32 - 96)
                        gm = ((k - 2) // SLOTS) % BODY
                        act.wait_ge(gates_staged, b + (1 if sl >= 2 else 0))
                        for i in range(UB):
                            col = 2 * ((sl + 2) % SLOTS) + i
                            nc.scalar.activation(og[:, k % 2, i], bank_o[:, i * D:(i + 1) * D], ACT.Copy,
                                                 scale=gate_st[:, gm, col:col + 1]).then_inc(og_done, 1)
                    if there(b, NB) and there(b + 1, NB):
                        if sl == 3:
                            skip_term((m + 1) % 2, (j * 2 + (m + 1) // 2 + 1) * 16, b * N + 1)
                        if sl == 2:
                            take_z(b + 2, (m + 1) % 2, 1)
                            softplus_exp(b + 2)
                    if sl == 3 and there(b - 1, NB):
                        take_yrow(0, b * 2 - 1, b * 16 - 16)
                    if there(u + 1, NU):
                        nd = ((k + 1) // SLOTS) % 2
                        decays((k + 1) % 2, nd, (sl + 1) % SLOTS, u * 4, b + (2 if sl == 3 else 1))
                        take_ext(k + 1, u + 2, u * 4)
                    if there(b, NB) and there(b + 1, NB):
                        if sl == 1:
                            take_mid(b + 2)
                        if sl == 2:
                            softplus_ln(b + 2)
                    if sl == 0 and there(u, NU - BU // 2):
                        round_w1(j * 2 + e2 + 1, (e2 + 1) % 2, m % 2, (u - k % 8) * 4)
                    if there(u, NU):
                        act.wait_ge(staged, j * 4 + 2 * e2 + 2)
                        wait(act, down_done, u - 1)
                        for f in range(FC):
                            if f % 2 == 0:
                                act.wait_ge(up_done, u * 4 + f // 2 + 1)
                            nc.scalar.activation(hid[:, k % 2, f], bank_l[f // 2][:, (f % 2) * UT:(f % 2 + 1) * UT],
                                                 ACT.Gelu_apprx_tanh, bias=b1_st[:, e2, f:f + 1]).then_inc(gelu_done, 1)
                    if there(b, NB) and there(b + 1, NB):
                        if sl == 0:
                            take_bc(b + 2)
                        if sl == 1:
                            take_z(b + 2, (m + 1) % 2, 0)
                    if sl == 3 and there(b - 1, NB):
                        take_yrow(1, b * 2, b * 16 - 16)

            both(main, NJ)(act)

        @block.vector
        def _(dve):
            nc.vector.memset(ones3[:], 1.0).then_inc(consts_set, 1)
            nc.vector.memset(wg_wide, 0.0).then_inc(wide_set, 1)
            dve.wait_ge(row_made, 1)
            nc.vector.tensor_scalar(row_i[:, 1:2], row_i[:, 0:1], P - E, (T // E).bit_length() - 1, ALU.bitwise_and,
                                    ALU.logical_shift_left).then_inc(row_made, 1)
            dve.wait_ge(row_made, 2)
            nc.vector.tensor_copy(row_f[:, 0:1], row_i[:, 1:2]).then_inc(row_made, 1)
            dve.wait_ge(row_made, 3)
            nc.vector.tensor_scalar(row_f[:, 1:2], row_f[:, 0:1], float(HALF * T), None, ALU.add).then_inc(row_made, 1)
            dve.wait_ge(params_in, 16 * 7)
            nc.vector.tensor_copy(b2_hi[:], b2_f).then_inc(b2_step, 1)
            dve.wait_ge(b2_step, 1)
            nc.vector.tensor_tensor(b2_f, b2_f, b2_hi[:], ALU.subtract).then_inc(b2_step, 1)
            dve.wait_ge(b2_step, 2)
            nc.vector.tensor_copy(b2_mid[:], b2_f).then_inc(b2_step, 1)
            dve.wait_ge(b2_step, 3)
            nc.vector.tensor_tensor(b2_f, b2_f, b2_mid[:], ALU.subtract).then_inc(b2_step, 1)
            dve.wait_ge(b2_step, 4)
            nc.vector.tensor_copy(b2_lo[:], b2_f).then_inc(b2_step, 1)
            dve.wait_ge(a_exp, 1)
            nc.vector.tensor_scalar(a_sb[:], a_sb[:], -1.0, None, ALU.mult).then_inc(a_made, 1)

            for hc in range(HC):
                for place in range(GATE):
                    dve.wait_ge(wide_set, 1)
                    nc.vector.tensor_copy(wg_wide[:, hc * GATE + place, place * E:(place + 1) * E], wg_sb[:, hc]).then_inc(wide_set, 1)

            def rows(q):
                for r in range(ROWS):
                    b = q * ROWS + r
                    i4 = r % 4
                    g, gp = q * 2 + r // GATE, (r // GATE + 1) % 2
                    first = r % GATE == 1 and there(g - 2, NB // GATE)
                    second = r % GATE == 3 and there(g - 2, NB // GATE)
                    gq = 1 - gp
                    lg = bank_t[:, 0:TC * GATE * E].rearrange("p (a e) -> p a e", e=E)
                    if r % GATE == 3 and there(g - 1, NB // GATE):
                        dve.wait_ge(logits_done, g * GATE)
                        wait(dve, lg_tr, g - 1)
                        nc.vector.tensor_copy(lgt, (bank_o, bank_c)[gp][0:GATE * E, :]).then_inc(lgt_done, 1)
                    if first:
                        dve.wait_ge(lg_tr, g - 1)
                        nc.vector.reduce_max(lmax[:, gq], lg, axis=AX.X).then_inc(lmax_done, 1)
                    if second:
                        dve.wait_ge(lexp_done, g - 1)
                        nc.vector.reduce_sum(lsum[:, gq], lexp[:, gq], axis=AX.X).then_inc(lnorm, 1)
                    if there(b, NB):
                        dve.wait_ge(x_in[i4], (q * 2 + r // 4) * 16 + 16)
                        for c in range(TC):
                            nc.vector.bn_stats(stats[:, i4, c], xin[:, i4, c]).then_inc(stats_done, 1)
                    if first:
                        dve.wait_ge(lmax_done, g - 1)
                        nc.vector.tensor_tensor(lsh[:, gq], lg, lmax[:, gq].unsqueeze(2).broadcast_to([P, TC * GATE, E]),
                                                ALU.subtract).then_inc(lsh_done, 1)
                    if second:
                        dve.wait_ge(lnorm, g * 2 - 3)
                        nc.vector.reciprocal(lrec[:, gq], lsum[:, gq]).then_inc(lnorm, 1)
                    if there(b - 1, NB):
                        dve.wait_ge(rstd_done, b)
                        wait(dve, xn_done, b - 4)
                        nc.vector.scalar_tensor_tensor(out=shift[:, (r - 1) % 4], in0=mv[:, (r - 1) % 4, :, 0], scalar=-1.0,
                                                       in1=rstd[:, (r - 1) % 4], op0=ALU.mult, op1=ALU.mult).then_inc(shift_done, 1)
                    if there(b, NB):
                        dve.wait_ge(stats_done, b * TC + TC)
                        dve.sem_inc(turn["dve"], 1)
                        for c in range(TC):
                            nc.vector.bn_aggr(mv[:, i4, c], stats[:, i4, c]).then_inc(mv_done, 1)
                    if second:
                        dve.wait_ge(lnorm, g * 2 - 2)
                        nc.vector.tensor_tensor(probs[:, :, bass.ds(g * GATE - 2 * GATE, GATE), :],
                                                lexp[:, gq].rearrange("p (c b) e -> p c b e", c=TC),
                                                lrec[:, gq].rearrange("p (c b) -> p c b", c=TC).unsqueeze(3).broadcast_to([P, TC, GATE, E]),
                                                ALU.mult).then_inc(probs_done, 1)
                    if there(b, NB):
                        dve.wait_ge(mv_done, b * TC + TC)
                        nc.vector.tensor_scalar(vare[:, i4], mv[:, i4, :, 1], EPS, None, ALU.add).then_inc(vare_done, 1)

            both(rows, NB // ROWS)(dve)

            def take_rest(nb):
                dve.wait_ge(hi_done, nb)
                wait(dve, lo_done, nb - 1)
                nc.vector.tensor_tensor(bc_rest[64:96, :], bank_t[64:96, :], bc_hi[64:96, :],
                                        ALU.subtract).then_inc(rest_done, 1)

            def take_lo(nb, par, used):
                dve.wait_ge(mid_done, nb)
                wait(dve, c_ready, used)
                nc.vector.tensor_tensor(bcs[64:96, par], bc_rest[64:96, :], bc_mid[64:96, :],
                                        ALU.subtract).then_inc(lo_done, 1)

            def ext_low(k, nu, used):
                dve.wait_ge(ext_hi_done, nu)
                wait(dve, up_done, used)
                nc.vector.tensor_tensor(ext_lo[:, k % 2], bank_t[:].rearrange("p (c t) -> p c t", c=HC),
                                        ext_hi[:, k % 2].bitcast(F32), ALU.subtract).then_inc(ext_lo_done, 1)

            def take_delta(nb, par):
                dve.wait_ge(sp_step, nb * 2)
                nc.vector.tensor_tensor(delta[:, par], delta[:, par], zabs[:], ALU.add).then_inc(delta_done, 1)

            def take_du(nb, par, loaded):
                dve.wait_ge(delta_done, nb)
                dve.wait_ge(xnt_in[par], loaded)
                nc.vector.tensor_tensor(du[:, par], delta[:, par], xnt[:, par], ALU.mult).then_inc(du_done, 1)

            take_rest(1)
            take_lo(1, 0, 0)
            def multiply_b(s, place, par, b):
                dve.wait_ge(b_ready, s + 1)
                dve.wait_ge(du_done, b + 1)
                wait(dve, prod_done, s - 1)
                nc.vector.tensor_tensor(state[:, place], du[:, par], bank_b[:][:, None, :].broadcast_to([P, HC, T]),
                                        ALU.mult).then_inc(bx_done, 1)

            ops, last = 0, [0, 0]

            def top_round(half, t):
                nonlocal ops
                v8, i8, w = vals[:, half, 8 * t:8 * t + 8], idx_u[:, half, 8 * t:8 * t + 8], work[:, half]
                if t:
                    dve.wait_ge(round_op, last[half])
                nc.vector.max(v8, w).then_inc(round_op, 1)
                dve.wait_ge(round_op, ops + 1)
                nc.vector.max_index(i8, v8, w).then_inc(round_op, 1)
                nc.vector.match_replace(w, v8, w, -1.0).then_inc(round_op, 1)
                ops += 3
                last[half] = ops

            def picks_numbered(half):
                dve.wait_ge(round_op, last[half])
                nc.vector.tensor_scalar(idx_f[:, half], idx_u[:, half], row_f[:, half:half + 1], None,
                                        ALU.add).then_inc(picks, 1)

            def picks_out(half):
                dve.wait_ge(picks_tr, half + 1)
                for dst, part in ((idx_all, 0), (gate_all, 1)):
                    nc.vector.tensor_copy(dst[:, half * P:(half + 1) * P].rearrange("p (e b) -> p b e", e=E),
                                          bank_l[3 * half][:, part * P:(part + 1) * P].rearrange("p (b e) -> p b e", e=E)
                                          ).then_inc(picks_done, 1)

            dve.wait_ge(row_made, 4)
            for half in range(2):
                dve.wait_ge(work_in, half + 1)
            for t in range(LEAD):
                top_round(0, t)
            for r in range(4):
                dve.wait_ge(rows_out[r], 16 * NB // 4)
            dve.wait_ge(xn_tr, NB)
            nc.vector.memset(decay[:, :, :, :, 0:1], 0.0).then_inc(zero_set, 1)
            take_delta(1, 0)
            top_round(1, 0)
            take_du(1, 0, 16)
            for t in range(LEAD, K // 8):
                top_round(0, t)
                if t > LEAD:
                    top_round(1, t - LEAD)
            picks_numbered(0)
            top_round(1, K // 8 - LEAD)
            picks_out(0)
            for t in range(K // 8 - LEAD + 1, K // 8):
                top_round(1, t)
            picks_numbered(1)
            multiply_b(0, 0, 0, 0)
            ext_low(0, 1, 0)
            picks_out(1)

            def main(j):
                for k in range(BU):
                    m, sl = k // SLOTS, k % SLOTS
                    u, b = j * BU + k, j * BODY + m
                    if not there(b, NB):
                        continue
                    par = m % 2
                    for i in range(STEPS):
                        n = sl * STEPS + i
                        s = b * N + n
                        if sl == 1 and i == 0 and there(b + 1, NB):
                            take_rest(b + 2)
                        dve.wait_ge(decay_done, s * 2 + 2)
                        dve.wait_ge(bx_done, s + 1)
                        h = state[:, i % 2].rearrange("p c t -> p (c t)")
                        nc.vector.tensor_tensor_scan(h, decay[:, k % 2, i].rearrange("p c t -> p (c t)"), h, 0.0,
                                                     ALU.mult, ALU.add).then_inc(scan_done, 1)
                        if there(s + 1, NB * N):
                            multiply_b(s + 1, (i + 1) % 2, par if n < N - 1 else 1 - par, b if n < N - 1 else b + 1)
                        dve.wait_ge(c_ready, s + 1)
                        wait(dve, sum_done, s - 3)
                        dve.wait_ge(scan_done, s + 1)
                        nc.vector.tensor_tensor(prod[:, i], state[:, i % 2], bank_c[:][:, None, :].broadcast_to([P, HC, T]),
                                                ALU.mult).then_inc(prod_done, 1)
                        if i == 2 and there(u + 1, NU):
                            ext_low(k + 1, u + 2, u * 4)
                        if sl == 1 and i == 3 and there(b + 1, NB):
                            take_lo(b + 2, (m + 1) % 2, b * N)
                        if sl == 2 and i == 3 and there(b + 1, NB):
                            take_delta(b + 2, (m + 1) % 2)
                        if sl == 3 and i == 0 and there(b + 1, NB):
                            take_du(b + 2, (m + 1) % 2, (j * 2 + (m + 1) // 2 + 1) * 16)

            both(main, NJ)(dve)

        @block.tensor
        def _(pe):
            pe.wait_ge(params_in, 16 * 7)
            pe.wait_ge(ident_made, 2)
            pe.wait_ge(wide_set, 1 + HC * GATE)

            def rows(q):
                for r in range(ROWS):
                    b = q * ROWS + r
                    par = r % 2
                    if there(b, NB):
                        pe.wait_ge(xn_done, b + 1)
                        wait(pe, xnt_done, b * 2 - 2)
                        for hc in range(HC):
                            for c in range(TC):
                                i = nc.tensor.transpose(bank_l[2 * par + hc][:, c * P:(c + 1) * P],
                                                        xno[:, r % 4, c, hc * P:(hc + 1) * P], ident[:])
                        i.then_inc(xn_tr, 1)
                    if there(b - 1, NB):
                        pp, place = (r - 1) % 2, (r - 1) % GATE
                        lg = (bank_o, bank_c)[(r - 1) // GATE % 2]
                        pe.wait_ge(xnt_done, b * 2)
                        if place == 0:
                            wait(pe, lgt_done, q * 2 + (r - 1) // GATE - 1)
                        for hc in range(HC):
                            i = nc.tensor.matmul(lg[0:GATE * E, :], wg_wide[:, hc * GATE + place], xtr[:, pp, hc],
                                                 start=(place == 0 and hc == 0), stop=(place == GATE - 1 and hc == HC - 1))
                        i.then_inc(logits_done, 1)
                    g = q * 2 + r // GATE
                    if r % GATE == 1 and there(g - 1, NB // GATE):
                        pe.wait_ge(lgt_done, g)
                        wait(pe, lsh_done, g - 1)
                        pe.sem_inc(turn["pe"], 1)
                        for c in range(TC):
                            i = nc.tensor.transpose(bank_t[:, c * GATE * E:(c + 1) * GATE * E], lgt[:, c * P:(c + 1) * P],
                                                    ident[0:GATE * E, 0:GATE * E])
                        i.then_inc(lg_tr, 1)

            both(rows, NB // ROWS)(pe)

            def project(nb, par, loaded):
                pe.wait_ge(xnt_in[par], loaded)
                for hc in range(HC):
                    i = nc.tensor.matmul(bank_t[0:BC, :], wdbc_sb[:, hc], xnt[:, par, hc],
                                         start=(hc == 0), stop=(hc == HC - 1))
                i.then_inc(bc_proj, 1)

            def expand(nb, dt):
                pe.wait_ge(low_done, nb)
                nc.tensor.matmul(bank_t[:], wdt_sb[:, dt * P:(dt + 1) * P], low[:], start=True, stop=True).then_inc(z_done, 1)

            def chosen_columns(k, count, taken):
                pe.wait_ge(gathered[k % 2], count)
                wait(pe, ext_lo_done, taken)
                for i in range(UB):
                    for hc in range(HC):
                        o = nc.tensor.transpose(bank_t[:, hc * UT + i * K:hc * UT + (i + 1) * K],
                                                ex[:, k % 2, i, hc * P:(hc + 1) * P], ident[:])
                o.then_inc(ex_tr, 1)

            def y_rows(par, half):
                for c in (2 * half, 2 * half + 1):
                    for dt in range(HC):
                        o = nc.tensor.transpose(bank_t[:, (c % 2) * D + dt * P:(c % 2) * D + (dt + 1) * P],
                                                ysum[:, par, dt, c * P:(c + 1) * P], ident[:])
                o.then_inc(y_tr, 1)

            def spread_b(s, n, par):
                wait(pe, bx_done, s)
                nc.tensor.matmul(bank_b[:], pick[:, n:n + 1].broadcast_to([3 * 2 * N, P]), bcs[:, par],
                                 start=True, stop=True).then_inc(b_ready, 1)

            def stack_whole(b):
                pe.wait_ge(hi_moved, b * 16 + 16)
                pe.wait_ge(mid_moved, b * 16 + 16)
                pe.wait_ge(lo_done, b + 1)

            pe.wait_ge(pick_made, 4)
            pe.wait_ge(consts_set, 2)
            pe.wait_ge(probs_done, NB // GATE)
            for half in range(2):
                for c in range(TC):
                    i = nc.tensor.transpose(bank_l[half][:, c * P:(c + 1) * P],
                                            probs[:, c, half * HALF:(half + 1) * HALF, :].rearrange("p b e -> p (b e)"), ident[:])
                i.then_inc(probs_tr, 1)
            project(1, 0, 16)
            pe.wait_ge(hi_done, 1)
            pe.wait_ge(rest_done, 1)
            expand(1, 0)
            pe.wait_ge(z_taken, 2)
            expand(1, 1)
            pe.wait_ge(work_in, 2)

            def picks_lines(half):
                pe.wait_ge(picks, half + 1)
                nc.tensor.transpose(bank_l[3 * half][:, 0:P], idx_f[:, half], ident[:])
                nc.tensor.transpose(bank_l[3 * half][:, P:2 * P], vals[:, half], ident[:]).then_inc(picks_tr, 1)

            picks_lines(0)
            stack_whole(0)
            spread_b(0, 0, 0)
            pe.wait_ge(z_taken, 4)
            chosen_columns(0, 32, 0)
            picks_lines(1)
            def main(j):
                for k in range(BU):
                    m, sl = k // SLOTS, k % SLOTS
                    u, b = j * BU + k, j * BODY + m
                    e2, le2 = k // 8, ((k - 1) // 8) % 2
                    for q in range(2 * STEPS):
                        s = u * STEPS + q // 2
                        n = sl * STEPS + q // 2
                        if there(b, NB):
                            if q % 2 == 0 and there(s + 1, NB * N):
                                if n == N - 1:
                                    stack_whole(b + 1)
                                spread_b(s + 1, (n + 1) % N, m % 2 if n < N - 1 else (m + 1) % 2)
                            if q % 2 == 1:
                                wait(pe, prod_done, s)
                                nc.tensor.matmul(bank_c[:], pick[:, N + n:N + n + 1].broadcast_to([3 * 2 * N, P]),
                                                 bcs[:, m % 2], start=True, stop=True).then_inc(c_ready, 1)
                        if q == 0 and sl == 2 and there(b, NB) and there(b + 1, NB):
                            pe.wait_ge(z_taken, b * 4 + 6)
                            expand(b + 2, 1)
                        if q == 0 and sl == 3 and there(b - 1, NB):
                            pe.wait_ge(sum_done, b * N)
                            y_rows((m - 1) % 2, 0)
                        if q == 2 and there(u + 1, NU):
                            if sl == 1 and there(b + 1, NB):
                                pe.wait_ge(low_done, b + 2)
                                pe.wait_ge(rest_done, b + 2)
                            if sl == 2 and there(b + 1, NB):
                                pe.wait_ge(z_taken, b * 4 + 8)
                            if sl == 3 and there(b - 1, NB):
                                pe.wait_ge(yrow_done, b * 2 - 1)
                            if sl == 0 and there(b - 2, NB):
                                pe.wait_ge(yrow_done, b * 2 - 2)
                            chosen_columns(k + 1, (j * 8 + (k + 1) // 2 + 1) * 32, u + 1)
                        if q < 4 and there(u, NU):
                            if q == 0:
                                pe.wait_ge(ext_lo_done, u + 1)
                                if k % 8 == 0:
                                    pe.wait_ge(w1_lo_done, (j * 2 + e2 + 1) * W1_PARTS)
                            wait(pe, gelu_done, u * 8 - 8 + 2 * q + 2)
                            if isinstance(u, int) and u == 0 and q == 0:
                                pe.wait_ge(picks_done, 2)
                            if isinstance(u, int) and u == 0 and q == 3:
                                pe.wait_ge(picks_done, 4)
                            for f in (2 * q, 2 * q + 1):
                                for hc in range(HC):
                                    for w, m_ in ((w1_hi, ext_hi), (w1_hi, ext_lo), (w1_lo, ext_hi)):
                                        i = nc.tensor.matmul(bank_l[q][:, (f % 2) * UT:(f % 2 + 1) * UT],
                                                             w[:, e2, hc, f * P:(f + 1) * P], m_[:, k % 2, hc],
                                                             start=(hc == 0 and w is w1_hi and m_ is ext_hi),
                                                             stop=(hc == HC - 1 and w is w1_lo))
                            i.then_inc(up_done, 1)
                        if q >= 4 and there(u - 1, NU):
                            if q == 4:
                                wait(pe, og_done, u * 2 - 2)
                                pe.wait_ge(gelu_done, u * 8)
                                if k % 8 == 1:
                                    pe.wait_ge(w2_in[e2], j * 16 + 16)
                                    pe.wait_ge(staged, j * 4 + 2 * e2 + 2)
                            c = (q - 4) // 2
                            o = bank_o[:, c * D:(c + 1) * D]
                            if q % 2 == 0:
                                nc.tensor.matmul(o, ones3[:], b2_st[:, le2], start=True, stop=False)
                            for f in range(4 * (q % 2), 4 * (q % 2) + 4):
                                i = nc.tensor.matmul(o, hid[:, (k - 1) % 2, f, c * K:(c + 1) * K], w2_sb[:, le2, f],
                                                     start=False, stop=(f == FC - 1))
                            if q == 7:
                                i.then_inc(down_done, 1)
                        if q == LATE:
                            if there(u + 1, NU):
                                pe.wait_ge(ext_lo_done, u + 2)
                            if there(u, NU) and there(b + 1, NB):
                                if sl == 0:
                                    project(b + 2, (m + 1) % 2, (j * 2 + (m + 1) // 2 + 1) * 16)
                                if sl == 1:
                                    expand(b + 2, 0)
                            if sl == 3 and there(b - 1, NB):
                                if not there(u + 1, NU):
                                    pe.wait_ge(yrow_done, b * 2 - 1)
                                y_rows((m - 1) % 2, 1)

            both(main, NJ)(pe)


_NAMES = ["x", "wdbc", "wdt", "bdt", "alog", "dpar", "wg", "w1", "b1", "w2", "b2"]


def kernel(**inputs):
    import concourse.bacc as _bacc
    from concourse.bass_utils import run_bass_kernel_spmd as _run

    g = {k: np.asarray(v) for k, v in inputs.items()}
    laid = {
        "x": g["L0_attn_x"],
        "wdbc": g["L0_attn_W_deltaBC"].T,
        "wdt": g["L0_attn_W_dt"].T,
        "bdt": g["L0_attn_b_dt"].reshape(HC, P).T,
        "alog": g["L0_attn_A_log"].reshape(HC, P, N).transpose(1, 0, 2),
        "dpar": g["L0_attn_D_param"].reshape(HC, P).T,
        "wg": g["L0_ffn_Wg"].T,
        "w1": g["L0_ffn_W1"],
        "b1": g["L0_ffn_b1"].reshape(E, FC, P).transpose(2, 0, 1).reshape(P, E * FC),
        "w2": g["L0_ffn_W2"],
        "b2": g["L0_ffn_b2"].reshape(1, E * D),
    }
    nc = _bacc.Bacc("TRN2", target_bir_lowering=False, num_devices=1)
    arrays, args = {}, []
    for name in _NAMES:
        a = np.ascontiguousarray(laid[name])
        arrays[f"in_{name}"] = a
        args.append(nc.dram_tensor(f"in_{name}", a.shape, mybir.dt.from_np(a.dtype), kind="ExternalInput").ap())
    out = nc.dram_tensor("out_0", (NB, T, D), F32, kind="ExternalOutput").ap()
    build(nc, *args, out)
    r = _run(nc, [arrays], core_ids=[0])
    return r.results[0]["out_0"]
```
